# Optimizing a Trainium2 kernel written in Bass

```python
import numpy as np
import jax
import jax.numpy as jnp

def _softmax(x, axis=-1):
    return jax.nn.softmax(x, axis=axis)

def _gelu(x):
    return jax.nn.gelu(x, approximate=True)

def _silu(x):
    return jax.nn.silu(x)

def _sigmoid(x):
    return jax.nn.sigmoid(x)

def _layernorm(x, axis=-1, eps=1e-05):
    m = jnp.mean(x, axis=axis, keepdims=True)
    v = jnp.var(x, axis=axis, keepdims=True)
    return (x - m) / jnp.sqrt(v + eps)

def _scatter_add(tgt, idx, src, axis=0):
    return tgt.at[idx].add(src)

def _segment_sum(src, seg, n):
    return jax.ops.segment_sum(src, seg, n)
kernel_name = 'mk_gnn_resnorm_d1_gnn_r16_6e1e0a'

def setup_inputs(seed: int=0):
    np.random.seed(seed)
    _w = jnp.asarray

    def _rec_inputs():
        import jax
        import jax.numpy as jnp
        _gk = jax.random.key(seed)
        x = -0.0008691 + 1 * jax.random.normal(jax.random.fold_in(_gk, 1), (3125, 128), jnp.float32)
        _s = jax.random.randint(jax.random.fold_in(_gk, 2), (50000,), 0, 3125, jnp.int32)
        _d = jax.random.randint(jax.random.fold_in(_gk, 3), (50000,), 0, 3125, jnp.int32)
        _loop = jnp.arange(3125, dtype=jnp.int32)
        src = jnp.concatenate([_s, _d, _loop])
        dst = jnp.concatenate([_d, _s, _loop])
        _o = jnp.argsort(dst, stable=True)
        src = src[_o]
        dst = dst[_o]
        return (x, src, dst)
    x, src, dst = _rec_inputs()

    def _L0_gnn_setup():
        import jax, jax.numpy as jnp
        import numpy as np
        N = 625
        E = 10000
        IN = 128
        H1, C1 = (4, 128)
        H2, C2 = (2, 128)

        def transformer_conv(x, src, dst, Wq, bq, Wk, bk, Wv, bv, Ws, bs, H, C, concat):
            n = x.shape[0]
            q = (x @ Wq + bq).reshape(n, H, C)
            k = (x @ Wk + bk).reshape(n, H, C)
            v = (x @ Wv + bv).reshape(n, H, C)
            alpha = jnp.einsum('ehc,ehc->eh', q[dst], k[src]) / jnp.sqrt(jnp.float32(C))
            amax = jax.ops.segment_max(alpha, dst, num_segments=n)
            amax = jax.lax.stop_gradient(jnp.where(jnp.isfinite(amax), amax, 0.0))
            p = jnp.exp(alpha - amax[dst])
            denom = jax.ops.segment_sum(p, dst, num_segments=n) + 1e-16
            out = jax.ops.segment_sum(p[:, :, None] * v[src], dst, num_segments=n)
            out = out / denom[:, :, None]
            out = out.reshape(n, H * C) if concat else out.mean(axis=1)
            return out + x @ Ws + bs
        key = jax.random.key(seed)
        ks = jax.random.split(key, 20)
        w = lambda k, s: jax.random.normal(k, s, jnp.float32) * 0.02
        inp = {'x': jax.random.normal(ks[0], (N, IN), jnp.float32), 'edge_index': jax.random.randint(ks[1], (2, E), 0, N, jnp.int32), 'Wq1': w(ks[2], (IN, H1 * C1)), 'bq1': w(ks[3], (H1 * C1,)), 'Wk1': w(ks[4], (IN, H1 * C1)), 'bk1': w(ks[5], (H1 * C1,)), 'Wv1': w(ks[6], (IN, H1 * C1)), 'bv1': w(ks[7], (H1 * C1,)), 'Ws1': w(ks[8], (IN, H1 * C1)), 'bs1': w(ks[9], (H1 * C1,)), 'Wq2': w(ks[10], (H1 * C1, H2 * C2)), 'bq2': w(ks[11], (H2 * C2,)), 'Wk2': w(ks[12], (H1 * C1, H2 * C2)), 'bk2': w(ks[13], (H2 * C2,)), 'Wv2': w(ks[14], (H1 * C1, H2 * C2)), 'bv2': w(ks[15], (H2 * C2,)), 'Ws2': w(ks[16], (H1 * C1, C2)), 'bs2': w(ks[17], (C2,))}
        return inp
    _L0_gnn_all = _L0_gnn_setup()
    _L0_gnn_in = {k: v for k, v in _L0_gnn_all.items() if k in ('Wq1', 'bq1', 'Wk1', 'bk1', 'Wv1', 'bv1', 'Ws1', 'bs1', 'Wq2', 'bq2', 'Wk2', 'bk2', 'Wv2', 'bv2', 'Ws2', 'bs2')}
    del _L0_gnn_all
    return {'x': x, 'src': src, 'dst': dst, 'L0_gnn_Wq1': _L0_gnn_in['Wq1'], 'L0_gnn_bq1': _L0_gnn_in['bq1'], 'L0_gnn_Wk1': _L0_gnn_in['Wk1'], 'L0_gnn_bk1': _L0_gnn_in['bk1'], 'L0_gnn_Wv1': _L0_gnn_in['Wv1'], 'L0_gnn_bv1': _L0_gnn_in['bv1'], 'L0_gnn_Ws1': _L0_gnn_in['Ws1'], 'L0_gnn_bs1': _L0_gnn_in['bs1'], 'L0_gnn_Wq2': _L0_gnn_in['Wq2'], 'L0_gnn_bq2': _L0_gnn_in['bq2'], 'L0_gnn_Wk2': _L0_gnn_in['Wk2'], 'L0_gnn_bk2': _L0_gnn_in['bk2'], 'L0_gnn_Wv2': _L0_gnn_in['Wv2'], 'L0_gnn_bv2': _L0_gnn_in['bv2'], 'L0_gnn_Ws2': _L0_gnn_in['Ws2'], 'L0_gnn_bs2': _L0_gnn_in['bs2']}

def reference(x, src, dst, L0_gnn_Wq1, L0_gnn_bq1, L0_gnn_Wk1, L0_gnn_bk1, L0_gnn_Wv1, L0_gnn_bv1, L0_gnn_Ws1, L0_gnn_bs1, L0_gnn_Wq2, L0_gnn_bq2, L0_gnn_Wk2, L0_gnn_bk2, L0_gnn_Wv2, L0_gnn_bv2, L0_gnn_Ws2, L0_gnn_bs2):
    import jax
    import jax.numpy as jnp

    def _L0_gnn_ref(x, edge_index, Wq1, bq1, Wk1, bk1, Wv1, bv1, Ws1, bs1, Wq2, bq2, Wk2, bk2, Wv2, bv2, Ws2, bs2):
        import jax, jax.numpy as jnp
        import numpy as np
        N = 625
        E = 10000
        IN = 128
        H1, C1 = (4, 128)
        H2, C2 = (2, 128)

        def transformer_conv(x, src, dst, Wq, bq, Wk, bk, Wv, bv, Ws, bs, H, C, concat):
            n = x.shape[0]
            q = (x @ Wq + bq).reshape(n, H, C)
            k = (x @ Wk + bk).reshape(n, H, C)
            v = (x @ Wv + bv).reshape(n, H, C)
            alpha = jnp.einsum('ehc,ehc->eh', q[dst], k[src]) / jnp.sqrt(jnp.float32(C))
            amax = jax.ops.segment_max(alpha, dst, num_segments=n)
            amax = jax.lax.stop_gradient(jnp.where(jnp.isfinite(amax), amax, 0.0))
            p = jnp.exp(alpha - amax[dst])
            denom = jax.ops.segment_sum(p, dst, num_segments=n) + 1e-16
            out = jax.ops.segment_sum(p[:, :, None] * v[src], dst, num_segments=n)
            out = out / denom[:, :, None]
            out = out.reshape(n, H * C) if concat else out.mean(axis=1)
            return out + x @ Ws + bs
        src, dst = (edge_index[0], edge_index[1])
        h = transformer_conv(x, src, dst, Wq1, bq1, Wk1, bk1, Wv1, bv1, Ws1, bs1, H1, C1, True)
        h = jax.nn.relu(h)
        out = transformer_conv(h, src, dst, Wq2, bq2, Wk2, bk2, Wv2, bv2, Ws2, bs2, H2, C2, False)
        return out
    edge_index = jnp.stack([src, dst])
    x = _layernorm(x + _L0_gnn_ref(x, edge_index, L0_gnn_Wq1, L0_gnn_bq1, L0_gnn_Wk1, L0_gnn_bk1, L0_gnn_Wv1, L0_gnn_bv1, L0_gnn_Ws1, L0_gnn_bs1, L0_gnn_Wq2, L0_gnn_bq2, L0_gnn_Wk2, L0_gnn_bk2, L0_gnn_Wv2, L0_gnn_bv2, L0_gnn_Ws2, L0_gnn_bs2), axis=-1)
    return x

_drawn_inputs = setup_inputs


def setup_inputs(seed=0):
    import zlib

    import numpy as np

    out = dict(_drawn_inputs(seed))
    spreads = {}
    factors = {'L0_gnn_Wq1': 8.0,
     'L0_gnn_bq1': 8.0,
     'L0_gnn_Wk1': 8.0,
     'L0_gnn_bk1': 64.0,
     'L0_gnn_Wv1': 4.489,
     'L0_gnn_bv1': 7.583,
     'L0_gnn_bs1': 8.0,
     'L0_gnn_Wq2': 8.0,
     'L0_gnn_bq2': 40.597,
     'L0_gnn_Wk2': 8.0,
     'L0_gnn_bk2': 64.0,
     'L0_gnn_bv2': 4.539,
     'L0_gnn_bs2': 2.871}
    for name, (base, spread) in spreads.items():
        noise = np.random.default_rng([zlib.crc32(name.encode()), seed]).standard_normal(out[name].shape)
        drawn = base * np.exp(spread * noise) if base else spread * noise
        out[name] = jnp.asarray(drawn.astype(out[name].dtype))
    for name, factor in factors.items():
        out[name] = (out[name] * factor).astype(out[name].dtype)
    return out
```

```python
from contextlib import ExitStack

import concourse.bass as bass
import concourse.mybir as mybir

F32 = mybir.dt.float32
F16 = mybir.dt.float16
BF16 = mybir.dt.bfloat16
I32 = mybir.dt.int32
ALU = mybir.AluOpType
ACT = mybir.ActivationFunctionType
AX = mybir.AxisListType
RMAX = bass.bass_isa.ReduceOp.max

N = 3125
TP = 125
NT = N // TP
C = 128
H1, H2 = 4, 2
E = 103125
CE = 125
NCH = E // CE
CG = 11
CP = NCH // CG
PT = 4
PW = PT * TP
PIECES = [(a, min(a + PW, N)) for a in range(0, N, PW)]
NP = len(PIECES)
MID = N // 2
PAD = -3.0 * N
SCALE = float(C) ** -0.5
TINY = 2.0 ** -60
NEG_SLOPE = 1e30
NO_EDGE = 1e28
EPS_DENOM = 1e-16
EPS_NORM = 1e-5


def wait(eng, sem, value):
    if not (isinstance(value, int) and value <= 0):
        eng.wait_ge(sem, value)


def tiles_of(p):
    return range(PIECES[p][0] // TP, PIECES[p][1] // TP)


def build(nc, x, src, dst, Wq1, bq1, Wk1, bk1, Wv1, bv1, Ws1, bs1,
          Wq2, bq2, Wk2, bk2, Wv2, bv2, Ws2, bs2, out):
    mask_dram = nc.dram_tensor("mask_scratch", (NT, TP, N), F32, kind="Internal").ap()
    hT_dram = nc.dram_tensor("hT_scratch", (NT, C, H1 * TP), F32, kind="Internal").ap()

    with ExitStack() as ctx:
        def sb(name, shape, dt=F32):
            return ctx.enter_context(nc.sbuf_tensor(name, shape, dt))

        ident = sb("ident", [C, C])
        xres = sb("xres", [TP, NT, C])
        with ExitStack() as lay:
            def sb1(name, shape, dt=F32):
                return lay.enter_context(nc.sbuf_tensor(name, shape, dt))

            layer1 = {
                "featT": sb1("xT", [C, NT, 1, TP]),
                "KT": sb1("KT1", [C, H1, N]),
                "V": sb1("V1", [TP, NT, H1 * C]),
                "Wq": sb1("Wq1_sb", [C, 1, H1 * C]),
                "Ws": sb1("Ws1_sb", [C, 1, H1 * C]),
                "bq": sb1("bq1_sb", [C, H1]),
                "bs": sb1("bs1_sb", [TP, H1 * C]),
            }
            mask_and_projections(nc, x, src, dst, Wk1, bk1, Wv1, bv1, Wq1, bq1, Ws1, bs1, bs2,
                                 ident, xres, layer1, mask_dram)
            attention(nc, 1, H1, 1, layer1, mask_dram, ident, hT_dram=hT_dram)
        with ExitStack() as lay:
            def sb2(name, shape, dt=F32):
                return lay.enter_context(nc.sbuf_tensor(name, shape, dt))

            layer2 = {
                "featT": sb2("hT", [C, NT, H1, TP]),
                "KT": sb2("KT2", [C, H2, N]),
                "V": sb2("V2", [TP, NT, H2 * C]),
                "Wq": sb2("Wq2_sb", [C, H1, H2 * C]),
                "Ws": sb2("Ws2_sb", [C, H1, C]),
                "bq": sb2("bq2_sb", [C, H2]),
            }
            y = sb2("y", [TP, NT, C])
            stats = sb2("stats", [TP, NT, 6])
            projections2(nc, Wk2, bk2, Wv2, bv2, Wq2, bq2, Ws2, layer2, hT_dram)
            attention(nc, 2, H2, H1, layer2, mask_dram, ident, xres=xres, y=y, stats=stats)
            layer_norm(nc, y, stats, out)


def mask_and_projections(nc, x, src, dst, Wk, bk, Wv, bv, Wq, bq, Ws, bs, bs2,
                         ident, xres, L, mask_dram):
    xT, KT, V = L["featT"], L["KT"], L["V"]
    with ExitStack() as ctx:
        def sb(name, shape, dt=F32):
            return ctx.enter_context(nc.sbuf_tensor(name, shape, dt))

        def sem(name):
            return ctx.enter_context(nc.semaphore(name))

        Wk_sb, Wv_sb = sb("Wk1_sb", [C, H1 * C]), sb("Wv1_sb", [C, H1 * C])
        bk_sb, bv_sb = sb("bk1_sb", [C, H1]), sb("bv1_sb", [TP, H1 * C])
        bs2_sb = sb("bs2_sb", [TP, C])
        ends_i = sb("ends_i", [CP, 2, CG * CE], I32)
        ends_f = sb("ends_f", [CP, 2, CG * CE])
        dstE, srcE = sb("dstE", [CE, NCH + 1]), sb("srcE", [CE, NCH + 1])
        nodes = sb("nodes", [CE, N], F16)
        dst_hot = sb("dst_hot", [CE, 2, TP], BF16)
        src_hot = sb("src_hot", [CE, 2, N], BF16)
        zeros = sb("zeros", [CE, TP], BF16)
        log_sb = sb("log_sb", [TP, N])
        neg_sb = sb("neg_sb", [TP, 2, PW])
        tiny = sb("tiny", [TP, 1])
        win = sb("win", [CP, NT, CG])
        chunk_id = sb("chunk_id", [CP, CG])
        dmin, dmax = sb("dmin", [CP, CG]), sb("dmax", [CP, CG])
        below, touch, cand = (sb(n, [CP, NT, CG]) for n in ("below", "touch", "cand"))
        span, span_all = sb("span", [CP, 2, NT]), sb("span_all", [CP, 2, NT])
        first_c, steps_f, ends_cum, zero_row = (sb(n, [1, NT]) for n in ("first_c", "steps_f", "ends_cum", "zero_row"))
        end_c = sb("end_c", [1, NT])
        steps_i = sb("steps_i", [1, NT], I32)
        starts_f, offs_f = sb("starts_f", [1, NT]), sb("offs_f", [1, NT])
        table = sb("table", [1, 3, NT], I32)

        bank = [ctx.enter_context(nc.psum_tensor(f"mask_bank{i}", [C, 512], F32)) for i in range(8)]

        s_ends = [sem("dst_loaded"), sem("src_loaded")]
        s_x, s_wk, s_wv, s_bias, s_late = (sem(n) for n in ("x_loaded", "wk_loaded", "wv_loaded", "bias_loaded", "late_loaded"))
        s_ident0, s_ident, s_const = sem("ident_zeroed"), sem("ident_ready"), sem("const_ready")
        s_dve = sem("dve_chain")
        s_xtp, s_xt = sem("xT_in_psum"), sem("xT_ready")
        s_kp, s_k = sem("key_in_psum"), sem("key_ready")
        s_vp, s_v = sem("value_in_psum"), sem("value_ready")
        s_ep, s_e = sem("ends_in_psum"), sem("ends_ready")
        s_span, s_all = sem("span_ready"), sem("span_reduced")
        s_table = sem("table_ready")
        s_hot, s_hot_free = sem("hot_ready"), sem("hot_free")
        s_cnt, s_cnt_free = sem("count_ready"), sem("count_free")
        s_neg, s_seen = sem("negative_ready"), sem("logarithm_seen")
        s_masked, s_stored = sem("mask_ready"), sem("mask_stored")

        def ends_in(eng, which, dram):
            eng.dma_start(ends_i[:, which, :], dram.rearrange("(p n) -> p n", p=CP)).then_inc(s_ends[which], 16)

        XG = 4
        x_groups = [range(a, min(a + XG, NT)) for a in range(0, NT, XG)]
        EG = 6
        e_groups = [(w, g, min(g + EG, CG)) for w in range(2) for g in range(0, CG, EG)]
        KB, VB, EB = (0, 1), (2, 3), (4, 5)

        with nc.Block() as block:
            @block.sync
            def _(sp):
                ends_in(sp, 0, dst)
                sp.dma_start(xres[:, :, :], x.rearrange("(t p) c -> p t c", p=TP)).then_inc(s_x, 16)
                ends_in(sp, 1, src)
                with sp.Fori(0, NT) as w:
                    sp.wait_ge(s_masked, (w + 1) * NP)
                    sp.dma_start(mask_dram[bass.ds(w, 1)].rearrange("a p n -> (a p) n"), log_sb[:, :]).then_inc(s_stored, 16)
                sp.wait_ge(s_stored, 16 * NT)

            @block.scalar
            def _(act):
                act.dma_start(Wk_sb[:, :], Wk).then_inc(s_wk, 16)
                act.dma_start(Wv_sb[:, :], Wv).then_inc(s_wv, 16)
                with nc.allow_non_contiguous_dma("small bias columns"):
                    act.dma_start(bk_sb[:, :], bk.rearrange("(h c) -> c h", c=C)).then_inc(s_bias, 16)
                    act.dma_start(L["bq"][:, :], bq.rearrange("(h c) -> c h", c=C)).then_inc(s_late, 16)
                act.dma_start(bv_sb[:, :], bv.partition_broadcast(TP)).then_inc(s_bias, 16)
                act.dma_start(bs2_sb[:, :], bs2.partition_broadcast(TP)).then_inc(s_bias, 16)
                act.dma_start(L["bs"][:, :], bs.partition_broadcast(TP)).then_inc(s_late, 16)
                act.dma_start(L["Wq"][:, 0, :], Wq).then_inc(s_late, 16)
                act.dma_start(L["Ws"][:, 0, :], Ws).then_inc(s_late, 16)
                for n, g in enumerate(x_groups):
                    act.wait_ge(s_xtp, n + 1)
                    act.copy(xT[:, g[0]:g[-1] + 1, 0, :].rearrange("c t n -> c (t n)"),
                             bank[EB[n % 2]][:, 0:len(g) * TP]).then_inc(s_xt, 1)
                act.wait_ge(s_bias, 48)
                for n in range(H1 * NP):
                    h, (a, b) = n // NP, PIECES[n % NP]
                    act.wait_ge(s_kp, n + 1)
                    act.activation(KT[:, h, a:b], bank[KB[n % 2]][:, 0:b - a], ACT.Identity,
                                   bias=bk_sb[:, h:h + 1]).then_inc(s_k, 1)
                act.wait_ge(s_late, 64)
                act.wait_ge(s_const, 3)
                with act.Fori(0, NT) as w:
                    act.wait_ge(s_stored, 16 * w)
                    for p, (a, b) in enumerate(PIECES):
                        act.wait_ge(s_cnt, NP * w + p + 1)
                        act.activation(log_sb[:, a:b], bank[p][0:TP, 0:b - a], ACT.Ln,
                                       bias=tiny[:, 0:1], scale=2.0).then_inc(s_cnt_free, 1)

            @block.gpsimd
            def _(pool):
                pool.memset(ident[:, :], 0.0).then_inc(s_ident0, 1)
                pool.wait_ge(s_ident0, 1)
                pool.affine_select(out=ident[:, :], in_=ident[:, :], compare_op=ALU.not_equal, fill=1.0, base=0,
                                   pattern=[[-1, C]], channel_multiplier=1).then_inc(s_ident, 1)
                pool.iota(win[:, :, :], [[TP, NT], [0, CG]], base=0, channel_multiplier=0,
                          allow_small_or_imprecise_dtypes=True).then_inc(s_const, 1)
                pool.iota(chunk_id[:, :], [[1, CG]], base=0, channel_multiplier=CG,
                          allow_small_or_imprecise_dtypes=True).then_inc(s_const, 1)
                pool.memset(tiny[:, :], TINY).then_inc(s_const, 1)
                pool.iota(nodes[:, :], [[1, N]], base=-MID, channel_multiplier=0,
                          allow_small_or_imprecise_dtypes=True).then_inc(s_const, 1)
                pool.wait_ge(s_span, 2)
                pool.partition_all_reduce(span_all[:, :, :].rearrange("p a t -> p (a t)"),
                                          span[:, :, :].rearrange("p a t -> p (a t)"), CP, RMAX).then_inc(s_all, 1)
                pool.wait_ge(s_bias, 48)
                pool.wait_ge(s_xtp, len(x_groups))
                pool.tensor_tensor(xres[:, :, :], xres[:, :, :],
                                   bs2_sb[:, :].unsqueeze(1).broadcast_to([TP, NT, C]), ALU.add).then_inc(s_const, 1)
                with pool.Fori(0, NT) as w:
                    for p, (a, b) in enumerate(PIECES):
                        pool.wait_ge(s_cnt_free, NP * (w + 1) + p + 1).then_inc(s_seen, 1)
                        pool.tensor_scalar(neg_sb[:, p % 2, 0:b - a], log_sb[:, a:b], 0.0, NEG_SLOPE, ALU.min,
                                           ALU.mult).then_inc(s_neg, 1)
                        pool.wait_ge(s_neg, NP * w + p + 1)
                        pool.tensor_tensor(log_sb[:, a:b], log_sb[:, a:b], neg_sb[:, p % 2, 0:b - a],
                                           ALU.add).then_inc(s_masked, 1)

            @block.vector
            def _(dve):
                chain = [0]

                def link(ins):
                    chain[0] += 1
                    ins.then_inc(s_dve, 1)
                    dve.wait_ge(s_dve, chain[0])

                dve.memset(zeros[:, :], 0.0).then_inc(s_hot_free, 2)
                dve.memset(zero_row[:, :], 0.0).then_inc(s_cnt_free, NP)
                dve.memset(dstE[:, NCH:NCH + 1], PAD)
                dve.memset(srcE[:, NCH:NCH + 1], PAD)
                for which in range(2):
                    dve.wait_ge(s_ends[which], 16)
                    link(dve.tensor_copy(ends_f[:, which, :], ends_i[:, which, :]))
                    if which == 0:
                        d = ends_f[:, 0, :].rearrange("p (g e) -> p g e", g=CG)
                        dve.tensor_reduce(dmin[:, :], d, AX.X, ALU.min)
                        link(dve.tensor_reduce(dmax[:, :], d, AX.X, ALU.max))
                dve.wait_ge(s_const, 2)
                lo = dmin[:, :].unsqueeze(1).broadcast_to([CP, NT, CG])
                hi = dmax[:, :].unsqueeze(1).broadcast_to([CP, NT, CG])
                ids = chunk_id[:, :].unsqueeze(1).broadcast_to([CP, NT, CG])
                link(dve.tensor_tensor(below[:, :, :], lo, win[:, :, :], ALU.subtract))
                link(dve.tensor_scalar(below[:, :, :], below[:, :, :], float(TP), None, ALU.is_lt))
                link(dve.tensor_tensor(touch[:, :, :], hi, win[:, :, :], ALU.subtract))
                link(dve.scalar_tensor_tensor(touch[:, :, :], touch[:, :, :], 0.0, below[:, :, :], ALU.is_ge, ALU.mult))
                link(dve.scalar_tensor_tensor(cand[:, :, :], ids, -float(NCH), touch[:, :, :], ALU.add, ALU.mult))
                dve.tensor_reduce(span[:, 0, :], cand[:, :, :], AX.X, ALU.min, negate=True).then_inc(s_span, 1)
                link(dve.scalar_tensor_tensor(below[:, :, :], ids, 1.0, touch[:, :, :], ALU.add, ALU.mult))
                dve.tensor_reduce(span[:, 1, :], below[:, :, :], AX.X, ALU.max).then_inc(s_span, 1)
                for n, (which, g0, g1) in enumerate(e_groups):
                    dve.wait_ge(s_ep, n + 1)
                    to = (dstE, srcE)[which][:, 0:NCH].rearrange("e (p g) -> e g p", g=CG)[:, g0:g1, :]
                    dve.tensor_scalar(to, bank[6 + n % 2][0:CE, 0:(g1 - g0) * CP].rearrange("e (g p) -> e g p", p=CP),
                                      -float(MID), None, ALU.add).then_inc(s_e, 1)
                dve.wait_ge(s_all, 1)
                link(dve.tensor_scalar(first_c[:, :], span_all[0:1, 0, :], -1.0, float(NCH), ALU.mult, ALU.add))
                link(dve.tensor_scalar(first_c[:, :], first_c[:, :], float(NCH - 1), None, ALU.min))
                link(dve.tensor_tensor(end_c[:, :], span_all[0:1, 1, :], first_c[:, :], ALU.subtract))
                link(dve.tensor_scalar(end_c[:, :], end_c[:, :], 1.0, 1.0, ALU.max, ALU.add))
                link(dve.tensor_copy(steps_i[:, :], end_c[:, :]))
                link(dve.tensor_scalar(steps_i[:, :], steps_i[:, :], 1, None, ALU.arith_shift_right))
                link(dve.tensor_copy(steps_f[:, :], steps_i[:, :]))
                link(dve.tensor_tensor_scan(ends_cum[:, :], steps_f[:, :], zero_row[:, :], 0.0, ALU.add, ALU.add))
                link(dve.tensor_tensor(starts_f[:, :], ends_cum[:, :], steps_f[:, :], ALU.subtract))
                link(dve.scalar_tensor_tensor(offs_f[:, :], starts_f[:, :], -2.0, first_c[:, :], ALU.mult, ALU.add))
                dve.tensor_copy(table[:, 0, :], starts_f[:, :]).then_inc(s_table, 1)
                dve.tensor_copy(table[:, 1, :], ends_cum[:, :]).then_inc(s_table, 1)
                dve.tensor_copy(table[:, 2, :], offs_f[:, :]).then_inc(s_table, 1)
                dve.wait_ge(s_bias, 48)
                for t in range(NT):
                    dve.wait_ge(s_vp, t + 1)
                    dve.tensor_tensor(V[:, t, :], bank[VB[t % 2]][0:TP, :], bv_sb[:, :], ALU.add).then_inc(s_v, 1)
                dve.wait_ge(s_const, 4)
                dve.wait_ge(s_e, len(e_groups))
                dve.wait_ge(s_table, 3)
                with dve.Fori(0, NT) as w:
                    j0 = dve.value_load(table[0:1, 0, bass.ds(w, 1)], min_val=0, max_val=NCH * NT)
                    j1 = dve.value_load(table[0:1, 1, bass.ds(w, 1)], min_val=1, max_val=NCH * NT)
                    off = dve.value_load(table[0:1, 2, bass.ds(w, 1)], min_val=-2 * NCH * NT, max_val=NCH)
                    with dve.Fori(j0, j1) as j:
                        for u in range(2):
                            c = nc.s_assert_within(2 * j + off + u, 0, NCH, skip_runtime_bounds_check_because=
                                                   "the table's chunks end at NCH, the pad column")
                            dve.wait_ge(s_hot_free, 2 * j + u + 1)
                            dve.tensor_scalar(dst_hot[:, u, :], nodes[:, bass.ds(w * TP, TP)], dstE[:, bass.ds(c, 1)],
                                              None, ALU.is_equal)
                            dve.tensor_scalar(src_hot[:, u, :], nodes[:, :], srcE[:, bass.ds(c, 1)],
                                              None, ALU.is_equal).then_inc(s_hot, 1)

            @block.tensor
            def _(pe):
                pe.wait_ge(s_ident, 1)
                for n, (which, g0, g1) in enumerate(e_groups):
                    pe.wait_ge(s_dve, 1 if which == 0 else 3)
                    wait(pe, s_e, n - 1)
                    for g in range(g0, g1):
                        last = pe.transpose(bank[6 + n % 2][0:CE, (g - g0) * CP:(g - g0 + 1) * CP],
                                            ends_f[:, which, g * CE:(g + 1) * CE], ident[0:CP, 0:CP])
                    last.then_inc(s_ep, 1)
                pe.wait_ge(s_x, 16)
                for n, g in enumerate(x_groups):
                    wait(pe, s_xt, n - 1)
                    for t in g:
                        last = pe.transpose(bank[EB[n % 2]][:, (t - g[0]) * TP:(t - g[0] + 1) * TP],
                                            xres[:, t, :], ident[0:TP, 0:TP])
                    last.then_inc(s_xtp, 1)
                pe.wait_ge(s_xt, len(x_groups))
                pe.wait_ge(s_wk, 16)
                pe.wait_ge(s_wv, 16)
                xT_all = xT[:, :, 0, :].rearrange("c t n -> c (t n)")
                for n in range(H1 * NP):
                    h, (a, b) = n // NP, PIECES[n % NP]
                    wait(pe, s_k, n - 1)
                    pe.matmul(bank[KB[n % 2]][:, 0:b - a], Wk_sb[:, h * C:(h + 1) * C], xT_all[:, a:b],
                              start=True, stop=True).then_inc(s_kp, 1)
                    if n < NT:
                        wait(pe, s_v, n - 1)
                        pe.matmul(bank[VB[n % 2]][0:TP, :], xT[:, n, 0, :], Wv_sb[:, :],
                                  start=True, stop=True).then_inc(s_vp, 1)
                pe.wait_ge(s_k, H1 * NP)
                pe.wait_ge(s_v, NT)
                pe.wait_ge(s_e, len(e_groups))
                pe.wait_ge(s_table, 3)
                with pe.Fori(0, NT) as w:
                    j0 = pe.value_load(table[0:1, 0, bass.ds(w, 1)], min_val=0, max_val=NCH * NT)
                    j1 = pe.value_load(table[0:1, 1, bass.ds(w, 1)], min_val=1, max_val=NCH * NT)
                    for p, (a, b) in enumerate(PIECES):
                        pe.wait_ge(s_cnt_free, NP * w + p + 1)
                        pe.matmul(bank[p][0:TP, 0:b - a], zeros[:, :], nodes[:, a:b].bitcast(BF16),
                                  start=True, stop=False, skip_group_check=True)
                    with pe.Fori(j0, j1) as j:
                        for u in range(2):
                            pe.wait_ge(s_hot, 2 * j + u + 1)
                            for p, (a, b) in enumerate(PIECES):
                                last = pe.matmul(bank[p][0:TP, 0:b - a], dst_hot[:, u, :], src_hot[:, u, a:b],
                                                 start=False, stop=False, skip_group_check=True)
                            last.then_inc(s_hot_free, 1)
                    for p, (a, b) in enumerate(PIECES):
                        pe.matmul(bank[p][0:TP, 0:b - a], zeros[:, :], nodes[:, a:b].bitcast(BF16),
                                  start=False, stop=True, skip_group_check=True).then_inc(s_cnt, 1)


def projections2(nc, Wk, bk, Wv, bv, Wq, bq, Ws, L, hT_dram):
    hT, KT, V = L["featT"], L["KT"], L["V"]
    with ExitStack() as ctx:
        def sb(name, shape, dt=F32):
            return ctx.enter_context(nc.sbuf_tensor(name, shape, dt))

        def sem(name):
            return ctx.enter_context(nc.semaphore(name))

        Wk_sb, Wv_sb = sb("Wk2_sb", [C, H1, H2 * C]), sb("Wv2_sb", [C, H1, H2 * C])
        bk_sb, bv_sb = sb("bk2_sb", [C, H2]), sb("bv2_sb", [TP, H2 * C])
        bank = [ctx.enter_context(nc.psum_tensor(f"proj_bank{i}", [C, 512], F32)) for i in range(4)]
        s_h = [sem(f"h_loaded{p}") for p in range(NP)]
        s_w, s_bias, s_late = sem("w2_loaded"), sem("bias2_loaded"), sem("late2_loaded")
        s_kp, s_k = sem("key2_in_psum"), sem("key2_ready")
        s_vp, s_v = sem("value2_in_psum"), sem("value2_ready")

        with nc.Block() as block:
            @block.sync
            def _(sp):
                for p in range(NP):
                    t0, t1 = tiles_of(p)[0], tiles_of(p)[-1] + 1
                    sp.dma_start(hT[:, t0:t1, :, :].rearrange("c t h n -> c t (h n)"),
                                 hT_dram[t0:t1].rearrange("t c n -> c t n")).then_inc(s_h[p], 16)

            @block.scalar
            def _(act):
                act.dma_start(Wk_sb[:, :, :], Wk.rearrange("(k c) n -> c k n", c=C)).then_inc(s_w, 16)
                act.dma_start(Wv_sb[:, :, :], Wv.rearrange("(k c) n -> c k n", c=C)).then_inc(s_w, 16)
                with nc.allow_non_contiguous_dma("small bias columns"):
                    act.dma_start(bk_sb[:, :], bk.rearrange("(h c) -> c h", c=C)).then_inc(s_bias, 16)
                    act.dma_start(L["bq"][:, :], bq.rearrange("(h c) -> c h", c=C)).then_inc(s_late, 16)
                act.dma_start(bv_sb[:, :], bv.partition_broadcast(TP)).then_inc(s_bias, 16)
                act.dma_start(L["Wq"][:, :, :], Wq.rearrange("(k c) n -> c k n", c=C)).then_inc(s_late, 16)
                act.dma_start(L["Ws"][:, :, :], Ws.rearrange("(k c) n -> c k n", c=C)).then_inc(s_late, 16)
                act.wait_ge(s_bias, 32)
                for n in range(H2 * NP):
                    h, (a, b) = n % H2, PIECES[n // H2]
                    act.wait_ge(s_kp, n + 1)
                    act.activation(KT[:, h, a:b], bank[n % 2][:, 0:b - a], ACT.Identity,
                                   bias=bk_sb[:, h:h + 1]).then_inc(s_k, 1)
                act.wait_ge(s_late, 48)

            @block.vector
            def _(dve):
                dve.wait_ge(s_bias, 32)
                for t in range(NT):
                    dve.wait_ge(s_vp, t + 1)
                    dve.tensor_tensor(V[:, t, :], bank[2 + t % 2][0:TP, 0:H2 * C], bv_sb[:, :], ALU.add).then_inc(s_v, 1)

            @block.tensor
            def _(pe):
                pe.wait_ge(s_w, 32)
                n = 0
                for p, (a, b) in enumerate(PIECES):
                    pe.wait_ge(s_h[p], 16)
                    t0, t1 = tiles_of(p)[0], tiles_of(p)[-1] + 1
                    for h in range(H2):
                        wait(pe, s_k, n - 1)
                        for k in range(H1):
                            last = pe.matmul(bank[n % 2][:, 0:b - a], Wk_sb[:, k, h * C:(h + 1) * C],
                                             hT[:, t0:t1, k, :], start=k == 0, stop=k == H1 - 1)
                        last.then_inc(s_kp, 1)
                        n += 1
                    for t in tiles_of(p):
                        wait(pe, s_v, t - 1)
                        for k in range(H1):
                            last = pe.matmul(bank[2 + t % 2][0:TP, 0:H2 * C], hT[:, t, k, :], Wv_sb[:, k, :],
                                             start=k == 0, stop=k == H1 - 1)
                        last.then_inc(s_vp, 1)


def attention(nc, layer, H, KC, L, mask_dram, ident, hT_dram=None, xres=None, y=None, stats=None):
    featT, KT, V, Wq, Ws, bq = (L[n] for n in ("featT", "KT", "V", "Wq", "Ws", "bq"))
    W = H * C if layer == 1 else C
    LA = 4
    with ExitStack() as ctx:
        def sb(name, shape, dt=F32):
            return ctx.enter_context(nc.sbuf_tensor(f"{name}_l{layer}", shape, dt))

        def bank(name):
            return ctx.enter_context(nc.psum_tensor(f"{name}_l{layer}", [C, 512], F32))

        def sem(name):
            return ctx.enter_context(nc.semaphore(f"{name}_l{layer}"))

        QT = sb("QT", [C, H, TP])
        bq_s = sb("bq_scaled", [C, H])
        mask = sb("mask", [TP, N])
        prob = sb("prob", [TP, 2, N])
        probT = sb("probT", [TP, NP, PW])
        feat_now = sb("feat_now", [C, KC, TP])
        skip = sb("skip", [TP, W])
        rows = sb("rows", [TP, W])
        rowsT = sb("rowsT", [C, H * TP])
        piece_max = sb("piece_max", [TP, 2, NP])
        neg_max = sb("neg_max", [TP, 2])
        total = sb("total", [TP, 2])
        denom, inv, weight = sb("denom", [TP, 1]), sb("inv", [TP, 1]), sb("weight", [TP, 1])

        S = [bank(f"score{i}") for i in range(2)]
        T = [bank(f"transposed{i}") for i in range(2)]
        O = [bank(f"output{i}") for i in range(2)]
        B_q, B_skip = bank("query"), bank("skip_rows")

        s_mask = [sem("mask_a"), sem("mask_b")]
        s_feat = sem("feat_ready")
        s_bq = sem("query_bias_ready")
        s_qp, s_q = sem("query_in_psum"), sem("query_ready")
        s_score, s_seen, s_masked = sem("score_ready"), sem("score_seen"), sem("score_masked")
        s_max, s_exp = sem("max_ready"), sem("exp_ready")
        s_tp = [sem("transposed_for_act"), sem("transposed_for_dve")]
        s_t = [sem("probT_by_act"), sem("probT_by_dve")]
        s_pv = sem("values_summed")
        s_out = sem("rows_ready")
        s_sp, s_skip = sem("skip_in_psum"), sem("skip_ready")
        s_rp, s_r, s_stored = sem("rowsT_in_psum"), sem("rowsT_ready"), sem("rowsT_stored")
        s_w0, s_w1, s_w2, s_half = sem("denom_ready"), sem("inverse_ready"), sem("weight_ready"), sem("half_sum_ready")
        per = (NP - NP // 2, NP // 2)

        def over_tiles(eng, body):
            body(0)
            with eng.Fori(1, NT - 1) as t:
                body(t)
            body(NT - 1)

        def is_last(t):
            return isinstance(t, int) and t == NT - 1

        def is_first(t):
            return isinstance(t, int) and t == 0

        with nc.Block() as block:
            @block.sync
            def _(sp):
                def load_mask(t, half):
                    a, b = ((0, PIECES[LA][0]), (PIECES[LA][0], N))[half]
                    sp.dma_start(mask[:, a:b], mask_dram[bass.ds(t, 1)].rearrange("a p n -> (a p) n")[:, a:b]
                                 ).then_inc(s_mask[half], 16)

                def store_rowsT(t):
                    sp.wait_ge(s_r, t + 1)
                    sp.dma_start(hT_dram[bass.ds(t, 1)].rearrange("a p n -> (a p) n"), rowsT[:, :]).then_inc(s_stored, 16)

                def tile(t):
                    if not is_last(t):
                        for half in range(2):
                            sp.wait_ge(s_masked, NP * (H * t + H - 1) + (LA, NP)[half])
                            load_mask(t + 1, half)
                    if layer == 1:
                        store_rowsT(t)

                load_mask(0, 0)
                load_mask(0, 1)
                over_tiles(sp, tile)
                if layer == 1:
                    sp.wait_ge(s_stored, 16 * NT)

            @block.gpsimd
            def _(pool):
                def tile(t):
                    wait(pool, s_sp, t)
                    pool.tensor_copy(feat_now[:, :, :].rearrange("c k n -> c (k n)"),
                                     featT[:, bass.ds(t, 1), :, :].rearrange("c a k n -> c (a k n)")).then_inc(s_feat, 1)

                over_tiles(pool, tile)

            @block.scalar
            def _(act):
                def query(n, h):
                    act.wait_ge(s_qp, n + 1)
                    act.activation(QT[:, h, :], B_q[:, 0:TP], ACT.Identity, bias=bq_s[:, h:h + 1],
                                   scale=SCALE).then_inc(s_q, 1)

                def tile(t):
                    for h in range(H):
                        s = t * H + h
                        act.wait_ge(s_max, s + 1)
                        act.activation(prob[:, h % 2, :], prob[:, h % 2, :], ACT.Exp, bias=neg_max[:, h % 2:h % 2 + 1],
                                       accum_out=total[:, h % 2:h % 2 + 1]).then_inc(s_exp, 1)
                        if not is_last(t):
                            query(H + s, h)
                        for p in range(0, NP, 2):
                            a, b = PIECES[p]
                            act.wait_ge(s_tp[0], per[0] * s + p // 2 + 1)
                            wait(act, s_pv, NP * (s - 1) + p + 1)
                            act.copy(probT[:, p, 0:b - a], T[0][0:TP, 0:b - a]).then_inc(s_t[0], 1)

                act.mul(bq_s[:, :], bq[:, :], SCALE).then_inc(s_bq, 1)
                act.wait_ge(s_bq, 1)
                for h in range(H):
                    query(h, h)
                over_tiles(act, tile)

            @block.vector
            def _(dve):
                def masked_scores(s, h, first_of_tile, t):
                    wait(dve, s_max, s - 1)
                    for p, (a, b) in enumerate(PIECES):
                        if first_of_tile and p in (0, LA):
                            dve.wait_ge(s_mask[p // LA], 16 * (t + 1))
                        dve.wait_ge(s_score, NP * s + p + 1).then_inc(s_seen, 1)
                        dve.tensor_tensor_reduce(out=prob[:, h % 2, a:b], in0=S[p % 2][0:TP, 0:b - a], in1=mask[:, a:b],
                                                 scale=1.0, scalar=-3.0e38, op0=ALU.add, op1=ALU.max,
                                                 accum_out=piece_max[:, h % 2, p:p + 1]).then_inc(s_masked, 1)
                    dve.wait_ge(s_masked, NP * (s + 1))
                    dve.tensor_reduce(neg_max[:, h % 2:h % 2 + 1], piece_max[:, h % 2, :], AX.X, ALU.max,
                                      negate=True).then_inc(s_max, 1)

                def rows_transposed(t):
                    dve.wait_ge(s_rp, t + 1)
                    wait(dve, s_stored, 16 * t)
                    dve.tensor_scalar(rowsT[:, :], B_skip[:, 0:H * TP], 0.0, None, ALU.max).then_inc(s_r, 1)

                def tile(t):
                    for h in range(H):
                        s = t * H + h
                        if not (is_last(t) and h == H - 1):
                            masked_scores(s + 1, (h + 1) % H, h == H - 1, t + 1)
                        if layer == 1 and h == 0 and not is_first(t):
                            rows_transposed(t - 1)
                        for p in range(1, NP, 2):
                            a, b = PIECES[p]
                            dve.wait_ge(s_tp[1], per[1] * s + p // 2 + 1)
                            wait(dve, s_pv, NP * (s - 1) + p + 1)
                            dve.tensor_copy(probT[:, p, 0:b - a], T[1][0:TP, 0:b - a]).then_inc(s_t[1], 1)
                        if h == 0:
                            dve.wait_ge(s_sp, t + 1)
                            add = L["bs"][:, :] if layer == 1 else xres[:, bass.ds(t, 1), :].rearrange("p a c -> p (a c)")
                            dve.tensor_tensor(skip[:, :], B_skip[0:TP, 0:W], add, ALU.add).then_inc(s_skip, 1)
                        dve.wait_ge(s_exp, s + 1)
                        dve.tensor_scalar(denom[:, :], total[:, h % 2:h % 2 + 1], 1.0 if layer == 1 else float(H2),
                                          EPS_DENOM, ALU.mult, ALU.add).then_inc(s_w0, 1)
                        dve.wait_ge(s_w0, s + 1)
                        dve.reciprocal(inv[:, :], denom[:, :]).then_inc(s_w1, 1)
                        dve.wait_ge(s_w1, s + 1)
                        dve.scalar_tensor_tensor(weight[:, :], neg_max[:, h % 2:h % 2 + 1], NO_EDGE, inv[:, :],
                                                 ALU.is_lt, ALU.mult).then_inc(s_w2, 1)
                        dve.wait_ge(s_w2, s + 1)
                        dve.wait_ge(s_skip, t + 1)
                        dve.wait_ge(s_pv, NP * (s + 1))
                        o = O[h % 2][0:TP, 0:C]
                        if layer == 1:
                            dve.scalar_tensor_tensor(rows[:, h * C:(h + 1) * C], o, weight[:, 0:1], skip[:, h * C:(h + 1) * C],
                                                     ALU.mult, ALU.add).then_inc(s_out, 1)
                        elif h == 0:
                            dve.scalar_tensor_tensor(rows[:, :], o, weight[:, 0:1], skip[:, :],
                                                     ALU.mult, ALU.add).then_inc(s_out, 1)
                        else:
                            dve.wait_ge(s_out, s)
                            yt = y[:, bass.ds(t, 1), :].rearrange("p a c -> p (a c)")
                            dve.scalar_tensor_tensor(yt, o, weight[:, 0:1], rows[:, :], ALU.mult, ALU.add).then_inc(s_out, 1)
                            dve.wait_ge(s_out, s + 1)
                            dve.bn_stats(stats[:, bass.ds(t, 1), :].rearrange("p a c -> p (a c)"), yt)

                masked_scores(0, 0, True, 0)
                over_tiles(dve, tile)
                if layer == 1:
                    rows_transposed(NT - 1)

            @block.tensor
            def _(pe):
                def query(n, t, h):
                    wait(pe, s_q, n)
                    for k in range(KC):
                        last = pe.matmul(B_q[:, 0:TP], Wq[:, k, h * C:(h + 1) * C],
                                         featT[:, bass.ds(t, 1), k, :].rearrange("c a n -> c (a n)"),
                                         start=k == 0, stop=k == KC - 1)
                    last.then_inc(s_qp, 1)

                def scores(s, h):
                    pe.wait_ge(s_q, s + 1)
                    for p, (a, b) in enumerate(PIECES):
                        back = (0, -1)[p] if p < 2 else p - 1
                        wait(pe, s_masked, NP * s + back)
                        pe.matmul(S[p % 2][0:TP, 0:b - a], QT[:, h, :], KT[:, h, a:b],
                                  start=True, stop=True).then_inc(s_score, 1)

                def skip_product(t):
                    pe.wait_ge(s_feat, t + 1)
                    if layer == 1:
                        wait(pe, s_r, t)
                    else:
                        wait(pe, s_skip, t)
                    for k in range(KC):
                        last = pe.matmul(B_skip[0:TP, 0:W], feat_now[:, k, :], Ws[:, k, :], start=k == 0, stop=k == KC - 1)
                    last.then_inc(s_sp, 1)

                def rows_transposed(t):
                    pe.wait_ge(s_out, H * (t + 1))
                    for h in range(H):
                        last = pe.transpose(B_skip[:, h * TP:(h + 1) * TP], rows[:, h * C:(h + 1) * C], ident[0:TP, 0:TP])
                    last.then_inc(s_rp, 1)

                def transposes(s, p, h):
                    wait(pe, s_t[p % 2], per[p % 2] * s + p // 2)
                    for i, t in enumerate(tiles_of(p)):
                        last = pe.transpose(T[p % 2][0:TP, i * TP:(i + 1) * TP], prob[:, h % 2, t * TP:(t + 1) * TP],
                                            ident[0:TP, 0:TP])
                    last.then_inc(s_tp[p % 2], 1)

                def values(s, p, h):
                    pe.wait_ge(s_t[p % 2], per[p % 2] * s + p // 2 + 1)
                    if p == 0:
                        wait(pe, s_out, s - 1)
                    for i, t in enumerate(tiles_of(p)):
                        last = pe.matmul(O[h % 2][0:TP, 0:C], probT[:, p, i * TP:(i + 1) * TP],
                                         V[:, t, h * C:(h + 1) * C], start=t == 0, stop=t == NT - 1)
                    last.then_inc(s_pv, 1)

                def tile(t):
                    for h in range(H):
                        s = t * H + h
                        if not (is_last(t) and h == H - 1):
                            scores(s + 1, (h + 1) % H)
                        if layer == 1 and h == 0 and not is_first(t):
                            rows_transposed(t - 1)
                        if not is_last(t):
                            query(H + s, t + 1, h)
                        pe.wait_ge(s_exp, s + 1)
                        for p in range(NP):
                            transposes(s, p, h)
                            if p > 0:
                                values(s, p - 1, h)
                            if p == 3 and h == 0:
                                skip_product(t)
                        values(s, NP - 1, h)

                for h in range(H):
                    query(h, 0, h)
                scores(0, 0)
                over_tiles(pe, tile)
                if layer == 1:
                    rows_transposed(NT - 1)


def layer_norm(nc, y, stats, out):
    with ExitStack() as ctx:
        moments = ctx.enter_context(nc.sbuf_tensor("moments", [TP, NT, 2], F32))
        dev = ctx.enter_context(nc.sbuf_tensor("dev", [TP, NT], F32))
        eps = ctx.enter_context(nc.sbuf_tensor("eps", [TP, 1], F32))
        s_eps, s_mom, s_dev, s_inv, s_y, s_outd = (ctx.enter_context(nc.semaphore(n)) for n in
                                             ("eps_ready", "moments_ready", "dev_ready", "inv_dev_ready", "y_ready", "out_stored"))
        with nc.Block() as block:
            @block.vector
            def _(dve):
                dve.memset(eps[:, :], EPS_NORM).then_inc(s_eps, 1)
                for t in range(NT):
                    dve.bn_aggr(moments[:, t, :], stats[:, t, :]).then_inc(s_mom, 1)
                dve.wait_ge(s_dev, 1)
                dve.reciprocal(dev[:, :], dev[:, :]).then_inc(s_inv, 1)
                dve.wait_ge(s_inv, 1)
                for t in range(NT):
                    dve.tensor_scalar(y[:, t, :], y[:, t, :], moments[:, t, 0:1], dev[:, t:t + 1],
                                      ALU.subtract, ALU.mult).then_inc(s_y, 1)

            @block.scalar
            def _(act):
                act.wait_ge(s_eps, 1)
                act.wait_ge(s_mom, NT)
                act.activation(dev[:, :], moments[:, :, 1], ACT.Sqrt, bias=eps[:, 0:1]).then_inc(s_dev, 1)

            @block.sync
            def _(sp):
                sp.wait_ge(s_y, NT)
                sp.dma_start(out.rearrange("(t p) c -> p t c", p=TP), y[:, :, :]).then_inc(s_outd, 16)
                sp.wait_ge(s_outd, 16)


_INS = ["x", "src", "dst"] + ["L0_gnn_" + a + b + n for n in "12" for a, b in
                              (("W", "q"), ("b", "q"), ("W", "k"), ("b", "k"), ("W", "v"), ("b", "v"), ("W", "s"), ("b", "s"))]


def kernel(**inputs):
    import numpy as _np
    import concourse.bacc as _bacc
    from concourse import mybir as _mybir
    from concourse.bass_utils import run_bass_kernel_spmd as _run

    nc = _bacc.Bacc("TRN2", target_bir_lowering=False, num_devices=1)
    arrays, args = {}, []
    for name in _INS:
        a = _np.ascontiguousarray(inputs[name])
        arrays[f"in_{name}"] = a
        args.append(nc.dram_tensor(f"in_{name}", a.shape, _mybir.dt.from_np(a.dtype), kind="ExternalInput").ap())
    args.append(nc.dram_tensor("out", (N, C), F32, kind="ExternalOutput").ap())
    build(nc, *args)
    r = _run(nc, [arrays], core_ids=[0])
    return r.results[0]["out"]
```

```python
from contextlib import ExitStack

import concourse.bass as bass
import concourse.mybir as mybir

F32 = mybir.dt.float32
F16 = mybir.dt.float16
BF16 = mybir.dt.bfloat16
I32 = mybir.dt.int32
ALU = mybir.AluOpType
ACT = mybir.ActivationFunctionType
AX = mybir.AxisListType
RMAX = bass.bass_isa.ReduceOp.max

N = 3125
TP = 125
NT = N // TP
C = 128
H1, H2 = 4, 2
E = 103125
CE = 125
NCH = E // CE
CG = 11
CP = NCH // CG
PT = 4
PW = PT * TP
PIECES = [(a, min(a + PW, N)) for a in range(0, N, PW)]
NP = len(PIECES)
ROW_SPLIT = ((0, 112), (112, TP))
SA = 5
SB = N // SA
NB = 2
WR = NB * TP
WD = WR // SA
NW = -(-N // (2 * WD)) * 2
HB = -(-SB // 2)
KF = 15
RING = 5
PAD = -1.0
BIG = 2.0 ** 100
SCALE = float(C) ** -0.5
TINY = 1e-30
NO_EDGE = 1e28
EPS_DENOM = 1e-16
EPS_NORM = 1e-5


def wait(eng, sem, value):
    if not (isinstance(value, int) and value <= 0):
        eng.wait_ge(sem, value)


def tiles_of(p):
    return range(PIECES[p][0] // TP, PIECES[p][1] // TP)


def build(nc, x, src, dst, Wq1, bq1, Wk1, bk1, Wv1, bv1, Ws1, bs1,
          Wq2, bq2, Wk2, bk2, Wv2, bv2, Ws2, bs2, out):
    mask_dram = nc.dram_tensor("mask_scratch", (NW * WD, N), F32, kind="Internal").ap()
    hT_dram = nc.dram_tensor("hT_scratch", (NT, C, H1 * TP), F32, kind="Internal").ap()

    with ExitStack() as ctx:
        def sb(name, shape, dt=F32):
            return ctx.enter_context(nc.sbuf_tensor(name, shape, dt))

        ident = sb("ident", [C, C])
        xres = sb("xres", [TP, NT, C])
        with ExitStack() as lay:
            def sb1(name, shape, dt=F32):
                return lay.enter_context(nc.sbuf_tensor(name, shape, dt))

            layer1 = {
                "featT": sb1("xT", [C, NT, 1, TP]),
                "KT": sb1("KT1", [C, H1, N]),
                "V": sb1("V1", [TP, NT, H1 * C]),
                "Wq": sb1("Wq1_sb", [C, 1, H1 * C]),
                "Ws": sb1("Ws1_sb", [C, 1, H1 * C]),
                "bq": sb1("bq1_sb", [C, H1]),
                "bs": sb1("bs1_sb", [TP, H1 * C]),
            }
            mask_and_projections(nc, x, src, dst, Wk1, bk1, Wv1, bv1, Wq1, bq1, Ws1, bs1, bs2,
                                 ident, xres, layer1, mask_dram)
            attention(nc, 1, H1, 1, layer1, mask_dram, ident, hT_dram=hT_dram)
        with ExitStack() as lay:
            def sb2(name, shape, dt=F32):
                return lay.enter_context(nc.sbuf_tensor(name, shape, dt))

            layer2 = {
                "featT": sb2("hT", [C, NT, H1, TP]),
                "KT": sb2("KT2", [C, H2, N]),
                "V": sb2("V2", [TP, NT, H2 * C]),
                "Wq": sb2("Wq2_sb", [C, H1, H2 * C]),
                "Ws": sb2("Ws2_sb", [C, H1, C]),
                "bq": sb2("bq2_sb", [C, H2]),
            }
            y = sb2("y", [TP, NT, C])
            stats = sb2("stats", [TP, NT, 6])
            projections2(nc, Wk2, bk2, Wv2, bv2, Wq2, bq2, Ws2, layer2, hT_dram)
            attention(nc, 2, H2, H1, layer2, mask_dram, ident, xres=xres, y=y, stats=stats)
            layer_norm(nc, y, stats, out)


def mask_and_projections(nc, x, src, dst, Wk, bk, Wv, bv, Wq, bq, Ws, bs, bs2,
                         ident, xres, L, mask_dram):
    xT, KT, V = L["featT"], L["KT"], L["V"]
    with ExitStack() as ctx:
        def sb(name, shape, dt=F32):
            return ctx.enter_context(nc.sbuf_tensor(name, shape, dt))

        def sem(name):
            return ctx.enter_context(nc.semaphore(name))

        Wk_sb, Wv_sb = sb("Wk1_sb", [C, H1 * C]), sb("Wv1_sb", [C, H1 * C])
        bk_sb, bv_sb = sb("bk1_sb", [C, H1]), sb("bv1_sb", [TP, H1 * C])
        bs2_sb = sb("bs2_sb", [TP, C])
        ends_i = sb("ends_i", [CP, 2, CG * CE], I32)
        ends_f = ends_i[:, :, :].bitcast(F32)
        dstE, srcE = sb("dstE", [CE, NCH]), sb("srcE", [CE, NCH])
        digit = sb("digit", [CE, NCH])
        row_of, col_of = sb("row_of", [CE, NCH + KF]), sb("col_of", [CE, NCH + KF])
        rows, cols = sb("rows", [CE, WR], F16), sb("cols", [CE, 2 * HB], F16)
        base = sb("base", [CE, NW])
        row_hot, col_hot = sb("row_hot", [CE, RING, WR], BF16), sb("col_hot", [CE, RING, 2 * HB], BF16)
        zeros = sb("zeros", [1, HB], BF16)
        tiny, big = sb("tiny", [TP, 1]), sb("big", [TP, 1])
        none, log = sb("none", [TP, NB, 2 * HB]), sb("log", [TP, NB, 2 * HB])
        win = sb("win", [CP, NW, CG])
        chunk_id = sb("chunk_id", [CP, CG])
        dmin, dmax = sb("dmin", [CP, CG]), sb("dmax", [CP, CG])
        below, touch = (sb(n, [CP, NW, CG]) for n in ("below", "touch"))
        span, span_all = sb("span", [CP, 2, NW]), sb("span_all", [CP, 2, NW])
        first_c, steps_f, ends_cum, zero_row = (sb(n, [1, NW]) for n in ("first_c", "steps_f", "ends_cum", "zero_row"))
        end_c = sb("end_c", [1, NW])
        steps_i = sb("steps_i", [1, NW], I32)
        starts_f, offs_f = sb("starts_f", [1, NW]), sb("offs_f", [1, NW])
        table = sb("table", [1, 3, NW], I32)
        first_i = sb("first_i", [1, NW], I32)
        most, few = sb("most", [1, 1]), sb("few", [1, 1], I32)

        banks = ctx.enter_context(nc.psum_tensor("mask_banks", [C, 8, 512], F32))
        bank = [banks[:, i, :] for i in range(4)]

        def counts(u, v):
            i = 2 * NB * u + 2 * v
            return banks[0:TP, i:i + 2, 0:HB]

        s_ends = [sem("dst_loaded"), sem("src_loaded")]
        s_x, s_wk, s_wv, s_bias, s_late = (sem(n) for n in ("x_loaded", "wk_loaded", "wv_loaded", "bias_loaded", "late_loaded"))
        s_ident0, s_ident, s_const = sem("ident_zeroed"), sem("ident_ready"), sem("const_ready")
        s_dve = sem("dve_chain")
        s_xtp, s_xt = sem("xT_in_psum"), sem("xT_ready")
        s_kp, s_k = sem("key_in_psum"), sem("key_ready")
        s_vp, s_v = sem("value_in_psum"), sem("value_ready")
        s_ep, s_e = sem("ends_in_psum"), sem("ends_ready")
        s_span, s_all = sem("span_ready"), sem("span_reduced")
        s_table = sem("table_ready")
        s_hot, s_hot_free = sem("hot_ready"), sem("hot_free")
        s_cnt = sem("count_in_psum")
        s_none, s_log, s_masked = sem("none_ready"), sem("logarithm_ready"), sem("mask_ready")
        s_stored = [sem("mask_stored_even"), sem("mask_stored_odd")]
        s_cols = sem("columns_ready")

        def ends_in(eng, which, dram):
            eng.dma_start(ends_i[:, which, :], dram.rearrange("(p n) -> p n", p=CP)).then_inc(s_ends[which], 16)

        XG = 4
        x_groups = [range(a, min(a + XG, NT)) for a in range(0, NT, XG)]
        EG = 6
        e_groups = [(w, g, min(g + EG, CG)) for w in range(2) for g in range(0, CG, EG)]
        KB, VB, EB = (0, 1), (2, 3), (0, 1)

        with nc.Block() as block:
            @block.sync
            def _(sp):
                ends_in(sp, 0, dst)
                sp.dma_start(xres[:, :, :], x.rearrange("(t p) c -> p t c", p=TP)).then_inc(s_x, 16)
                ends_in(sp, 1, src)
                blocks = mask_dram.rearrange("(w j) (a b) -> w (j a) b", j=TP // SA, a=SA)
                with sp.Fori(0, NW) as w:
                    for v in range(NB):
                        sp.wait_ge(s_masked, NB * w + v + 1)
                        for r0, r1 in ROW_SPLIT:
                            sp.dma_start(blocks[bass.ds(NB * w + v, 1), r0:r1, :].rearrange("w p b -> (w p) b"),
                                         log[r0:r1, v, 0:SB]).then_inc(s_stored[v], 16)
                for v in range(NB):
                    sp.wait_ge(s_stored[v], 16 * len(ROW_SPLIT) * NW)

            @block.scalar
            def _(act):
                act.dma_start(Wk_sb[:, :], Wk).then_inc(s_wk, 16)
                act.dma_start(Wv_sb[:, :], Wv).then_inc(s_wv, 16)
                with nc.allow_non_contiguous_dma("small bias columns"):
                    act.dma_start(bk_sb[:, :], bk.rearrange("(h c) -> c h", c=C)).then_inc(s_bias, 16)
                    act.dma_start(L["bq"][:, :], bq.rearrange("(h c) -> c h", c=C)).then_inc(s_late, 16)
                act.dma_start(bv_sb[:, :], bv.partition_broadcast(TP)).then_inc(s_bias, 16)
                act.dma_start(bs2_sb[:, :], bs2.partition_broadcast(TP)).then_inc(s_bias, 16)
                act.dma_start(L["bs"][:, :], bs.partition_broadcast(TP)).then_inc(s_late, 16)
                act.dma_start(L["Wq"][:, 0, :], Wq).then_inc(s_late, 16)
                act.dma_start(L["Ws"][:, 0, :], Ws).then_inc(s_late, 16)
                for n, g in enumerate(x_groups):
                    act.wait_ge(s_xtp, n + 1)
                    act.copy(xT[:, g[0]:g[-1] + 1, 0, :].rearrange("c t n -> c (t n)"),
                             bank[EB[n % 2]][:, 0:len(g) * TP]).then_inc(s_xt, 1)
                act.wait_ge(s_bias, 48)
                for n in range(H1 * NP):
                    h, (a, b) = n // NP, PIECES[n % NP]
                    act.wait_ge(s_kp, n + 1)
                    act.activation(KT[:, h, a:b], bank[KB[n % 2]][:, 0:b - a], ACT.Identity,
                                   bias=bk_sb[:, h:h + 1]).then_inc(s_k, 1)
                act.wait_ge(s_late, 64)
                act.wait_ge(s_const, 5)
                with act.Fori(0, NW // 2) as i:
                    for u in range(2):
                        act.wait_ge(s_cnt, 2 * i + u + 1)
                        for v in range(NB):
                            n = 2 * i + u
                            act.wait_ge(s_stored[v], 16 * len(ROW_SPLIT) * n)
                            act.activation(none[:, v, :].rearrange("p (a b) -> p a b", a=2), counts(u, v), ACT.Relu,
                                           bias=big[:, 0:1], scale=-BIG).then_inc(s_none, 1)
                            act.activation(log[:, v, :].rearrange("p (a b) -> p a b", a=2), counts(u, v), ACT.Ln,
                                           bias=tiny[:, 0:1]).then_inc(s_log, 1)

            @block.gpsimd
            def _(pool):
                pool.memset(ident[:, :], 0.0).then_inc(s_ident0, 1)
                pool.wait_ge(s_ident0, 1)
                pool.affine_select(out=ident[:, :], in_=ident[:, :], compare_op=ALU.not_equal, fill=1.0, base=0,
                                   pattern=[[-1, C]], channel_multiplier=1).then_inc(s_ident, 1)
                pool.iota(win[:, :, :], [[WD, NW], [0, CG]], base=0, channel_multiplier=0,
                          allow_small_or_imprecise_dtypes=True).then_inc(s_const, 1)
                pool.iota(chunk_id[:, :], [[1, CG]], base=0, channel_multiplier=CG,
                          allow_small_or_imprecise_dtypes=True).then_inc(s_const, 1)
                pool.iota(base[:, :], [[-WR, NW]], base=0, channel_multiplier=0,
                          allow_small_or_imprecise_dtypes=True).then_inc(s_const, 1)
                pool.memset(tiny[:, :], TINY).then_inc(s_const, 1)
                pool.memset(big[:, :], BIG).then_inc(s_const, 1)
                pool.iota(rows[:, :], [[1, WR]], base=0, channel_multiplier=0,
                          allow_small_or_imprecise_dtypes=True).then_inc(s_const, 1)
                pool.iota(cols[:, :], [[1, 2 * HB]], base=0, channel_multiplier=0,
                          allow_small_or_imprecise_dtypes=True).then_inc(s_const, 1)
                pool.wait_ge(s_span, 2)
                pool.partition_all_reduce(span_all[:, :, :].rearrange("p a t -> p (a t)"),
                                          span[:, :, :].rearrange("p a t -> p (a t)"), CP, RMAX).then_inc(s_all, 1)
                pool.wait_ge(s_bias, 48)
                pool.wait_ge(s_xtp, len(x_groups))
                pool.tensor_tensor(xres[:, :, :], xres[:, :, :],
                                   bs2_sb[:, :].unsqueeze(1).broadcast_to([TP, NT, C]), ALU.add).then_inc(s_const, 1)
                with pool.Fori(0, NW) as w:
                    for v in range(NB):
                        pool.wait_ge(s_log, NB * (w + 2) + v + 1)
                        pool.tensor_tensor(log[:, v, :], log[:, v, :], none[:, v, :], ALU.subtract).then_inc(s_masked, 1)

            @block.vector
            def _(dve):
                chain = [0]

                def link(ins):
                    chain[0] += 1
                    ins.then_inc(s_dve, 1)
                    dve.wait_ge(s_dve, chain[0])

                dve.memset(zeros[:, :], 0.0).then_inc(s_hot_free, RING)
                dve.memset(row_of[:, NCH:NCH + KF], PAD)
                dve.memset(col_of[:, NCH:NCH + KF], PAD)
                dve.memset(zero_row[:, :], 0.0).then_inc(s_log, 2 * NB)
                for which in range(2):
                    dve.wait_ge(s_ends[which], 16)
                    link(dve.tensor_copy(ends_f[:, which, :], ends_i[:, which, :]))
                for n, (which, g0, g1) in enumerate(e_groups):
                    dve.wait_ge(s_ep, n + 1)
                    to = (dstE, srcE)[which][:, :].rearrange("e (p g) -> e g p", g=CG)[:, g0:g1, :]
                    dve.tensor_copy(to, bank[EB[n % 2]][0:CE, 0:(g1 - g0) * CP].rearrange("e (g p) -> e g p", p=CP)
                                    ).then_inc(s_e, 1)
                d = ends_f[:, 0, :].rearrange("p (g e) -> p g e", g=CG)
                dve.tensor_reduce(dmin[:, :], d, AX.X, ALU.min)
                link(dve.tensor_reduce(dmax[:, :], d, AX.X, ALU.max))
                dve.wait_ge(s_const, 2)
                lo = dmin[:, :].unsqueeze(1).broadcast_to([CP, NW, CG])
                hi = dmax[:, :].unsqueeze(1).broadcast_to([CP, NW, CG])
                ids = chunk_id[:, :].unsqueeze(1).broadcast_to([CP, NW, CG])
                link(dve.tensor_tensor(below[:, :, :], lo, win[:, :, :], ALU.subtract))
                link(dve.tensor_scalar(below[:, :, :], below[:, :, :], float(WD), None, ALU.is_lt))
                link(dve.tensor_tensor(touch[:, :, :], hi, win[:, :, :], ALU.subtract))
                link(dve.scalar_tensor_tensor(touch[:, :, :], touch[:, :, :], 0.0, below[:, :, :], ALU.is_ge, ALU.mult))
                link(dve.scalar_tensor_tensor(below[:, :, :], ids, -float(NCH), touch[:, :, :], ALU.add, ALU.mult))
                link(dve.tensor_reduce(span[:, 0, :], below[:, :, :], AX.X, ALU.min, negate=True))
                link(dve.scalar_tensor_tensor(below[:, :, :], ids, 1.0, touch[:, :, :], ALU.add, ALU.mult))
                dve.tensor_reduce(span[:, 1, :], below[:, :, :], AX.X, ALU.max).then_inc(s_span, 2)
                dve.wait_ge(s_e, len(e_groups))
                link(dve.tensor_scalar(digit[:, :], srcE[:, :], float(SB), None, ALU.is_ge))
                for a in range(2, SA):
                    link(dve.scalar_tensor_tensor(digit[:, :], srcE[:, :], float(a * SB), digit[:, :], ALU.is_ge, ALU.add))
                dve.scalar_tensor_tensor(row_of[:, 0:NCH], dstE[:, :], float(SA), digit[:, :], ALU.mult, ALU.add
                                         ).then_inc(s_cols, 1)
                dve.scalar_tensor_tensor(col_of[:, 0:NCH], digit[:, :], -float(SB), srcE[:, :], ALU.mult, ALU.add
                                         ).then_inc(s_cols, 1)
                dve.wait_ge(s_bias, 48)
                for t in range(NT):
                    dve.wait_ge(s_vp, t + 1)
                    dve.tensor_tensor(V[:, t, :], bank[VB[t % 2]][0:TP, :], bv_sb[:, :], ALU.add).then_inc(s_v, 1)
                dve.wait_ge(s_all, 1)
                link(dve.tensor_scalar(first_c[:, :], span_all[0:1, 0, :], -1.0, float(NCH), ALU.mult, ALU.add))
                link(dve.tensor_scalar(first_c[:, :], first_c[:, :], float(NCH - 1), None, ALU.min))
                link(dve.tensor_tensor(end_c[:, :], span_all[0:1, 1, :], first_c[:, :], ALU.subtract))
                dve.tensor_copy(first_i[:, :], first_c[:, :]).then_inc(s_table, 1)
                link(dve.tensor_reduce(most[:, :], end_c[:, :], AX.X, ALU.max))
                dve.tensor_scalar(few[:, :], most[:, :], float(KF), None, ALU.is_le).then_inc(s_table, 1)
                link(dve.tensor_scalar(end_c[:, :], end_c[:, :], 1.0, 1.0, ALU.max, ALU.add))
                link(dve.tensor_copy(steps_i[:, :], end_c[:, :]))
                link(dve.tensor_scalar(steps_i[:, :], steps_i[:, :], 1, None, ALU.arith_shift_right))
                link(dve.tensor_copy(steps_f[:, :], steps_i[:, :]))
                link(dve.tensor_tensor_scan(ends_cum[:, :], steps_f[:, :], zero_row[:, :], 0.0, ALU.add, ALU.add))
                link(dve.tensor_tensor(starts_f[:, :], ends_cum[:, :], steps_f[:, :], ALU.subtract))
                link(dve.scalar_tensor_tensor(offs_f[:, :], starts_f[:, :], -2.0, first_c[:, :], ALU.mult, ALU.add))
                dve.tensor_copy(table[:, 0, :], starts_f[:, :]).then_inc(s_table, 1)
                dve.tensor_copy(table[:, 1, :], ends_cum[:, :]).then_inc(s_table, 1)
                dve.tensor_copy(table[:, 2, :], offs_f[:, :]).then_inc(s_table, 1)
                dve.wait_ge(s_const, 7)
                dve.wait_ge(s_cols, 2)
                dve.wait_ge(s_table, 5)

                def one_hot(u, row, col, w):
                    dve.tensor_scalar(row_hot[:, u, :], rows[:, :], row, base[:, bass.ds(w, 1)],
                                      ALU.subtract, ALU.is_equal)
                    dve.tensor_scalar(col_hot[:, u, :], cols[:, :], col, None, ALU.is_equal).then_inc(s_hot, 1)

                is_few = dve.value_load(few[0:1, 0:1], min_val=0, max_val=1)
                with dve.If(is_few > 0):
                    with dve.Fori(0, NW) as w:
                        c0 = nc.s_assert_within(dve.value_load(first_i[0:1, bass.ds(w, 1)]), 0, NCH - 1,
                                                skip_runtime_bounds_check_because="a chunk's number")
                        row_w, col_w = row_of[:, bass.ds(c0, KF)], col_of[:, bass.ds(c0, KF)]
                        for k in range(KF):
                            dve.wait_ge(s_hot_free, KF * w + k + 1)
                            one_hot(k % RING, row_w[:, k:k + 1], col_w[:, k:k + 1], w)
                with dve.Else():
                    with dve.Fori(0, NW) as w:
                        j0 = dve.value_load(table[0:1, 0, bass.ds(w, 1)], min_val=0, max_val=NCH * NW)
                        j1 = dve.value_load(table[0:1, 1, bass.ds(w, 1)], min_val=1, max_val=NCH * NW)
                        off = dve.value_load(table[0:1, 2, bass.ds(w, 1)], min_val=-2 * NCH * NW, max_val=NCH)
                        with dve.Fori(j0, j1) as j:
                            for u in range(2):
                                c = nc.s_assert_within(2 * j + off + u, 0, NCH, skip_runtime_bounds_check_because=
                                                       "the table's chunks end at NCH, the first pad column")
                                dve.wait_ge(s_hot_free, 2 * j + u + 1 + RING - 2)
                                one_hot(u, row_of[:, bass.ds(c, 1)], col_of[:, bass.ds(c, 1)], w)

            @block.tensor
            def _(pe):
                pe.wait_ge(s_ident, 1)
                for n, (which, g0, g1) in enumerate(e_groups):
                    pe.wait_ge(s_dve, 1 + which)
                    wait(pe, s_e, n - 1)
                    for g in range(g0, g1):
                        last = pe.transpose(bank[EB[n % 2]][0:CE, (g - g0) * CP:(g - g0 + 1) * CP],
                                            ends_f[:, which, g * CE:(g + 1) * CE], ident[0:CP, 0:CP])
                    last.then_inc(s_ep, 1)
                pe.wait_ge(s_x, 16)
                pe.wait_ge(s_e, len(e_groups))
                for n, g in enumerate(x_groups):
                    wait(pe, s_xt, n - 1)
                    for t in g:
                        last = pe.transpose(bank[EB[n % 2]][:, (t - g[0]) * TP:(t - g[0] + 1) * TP],
                                            xres[:, t, :], ident[0:TP, 0:TP])
                    last.then_inc(s_xtp, 1)
                pe.wait_ge(s_xt, len(x_groups))
                pe.wait_ge(s_wk, 16)
                pe.wait_ge(s_wv, 16)
                xT_all = xT[:, :, 0, :].rearrange("c t n -> c (t n)")
                for n in range(H1 * NP):
                    h, (a, b) = n // NP, PIECES[n % NP]
                    wait(pe, s_k, n - 1)
                    pe.matmul(bank[KB[n % 2]][:, 0:b - a], Wk_sb[:, h * C:(h + 1) * C], xT_all[:, a:b],
                              start=True, stop=True).then_inc(s_kp, 1)
                    if n < NT:
                        wait(pe, s_v, n - 1)
                        pe.matmul(bank[VB[n % 2]][0:TP, :], xT[:, n, 0, :], Wv_sb[:, :],
                                  start=True, stop=True).then_inc(s_vp, 1)
                pe.wait_ge(s_k, H1 * NP)
                pe.wait_ge(s_v, NT)
                pe.wait_ge(s_table, 5)

                def product(u, hot, first):
                    for v in range(NB):
                        for a in range(2):
                            ins = pe.matmul(counts(u, v)[:, a, :], row_hot[:, hot, v * TP:(v + 1) * TP],
                                            col_hot[:, hot, a * HB:(a + 1) * HB], start=first, stop=False,
                                            skip_group_check=True)
                    ins.then_inc(s_hot_free, 1)

                def add_zeros(u, width, first):
                    for v in range(NB):
                        for a in range(2):
                            ins = pe.matmul(counts(u, v)[:, a, 0:width], zeros[:, 0:TP], zeros[:, 0:width], start=first,
                                            stop=not first, skip_group_check=True)
                    return ins

                is_few = pe.value_load(few[0:1, 0:1], min_val=0, max_val=1)
                with pe.If(is_few > 0):
                    with pe.Fori(0, NW // 2) as i:
                        for u in range(2):
                            w = 2 * i + u
                            pe.wait_ge(s_log, NB * w + NB)
                            for k in range(KF):
                                pe.wait_ge(s_hot, KF * w + k + 1)
                                product(u, k % RING, k == 0)
                            add_zeros(u, 1, False).then_inc(s_cnt, 1)
                with pe.Else():
                    with pe.Fori(0, NW // 2) as i:
                        for u in range(2):
                            w = 2 * i + u
                            j0 = pe.value_load(table[0:1, 0, bass.ds(w, 1)], min_val=0, max_val=NCH * NW)
                            j1 = pe.value_load(table[0:1, 1, bass.ds(w, 1)], min_val=1, max_val=NCH * NW)
                            pe.wait_ge(s_log, NB * w + NB)
                            add_zeros(u, HB, True)
                            with pe.Fori(j0, j1) as j:
                                for hot in range(2):
                                    pe.wait_ge(s_hot, 2 * j + hot + 1)
                                    product(u, hot, False)
                            add_zeros(u, 1, False).then_inc(s_cnt, 1)


def projections2(nc, Wk, bk, Wv, bv, Wq, bq, Ws, L, hT_dram):
    hT, KT, V = L["featT"], L["KT"], L["V"]
    with ExitStack() as ctx:
        def sb(name, shape, dt=F32):
            return ctx.enter_context(nc.sbuf_tensor(name, shape, dt))

        def sem(name):
            return ctx.enter_context(nc.semaphore(name))

        Wk_sb, Wv_sb = sb("Wk2_sb", [C, H1, H2 * C]), sb("Wv2_sb", [C, H1, H2 * C])
        bk_sb, bv_sb = sb("bk2_sb", [C, H2]), sb("bv2_sb", [TP, H2 * C])
        bank = [ctx.enter_context(nc.psum_tensor(f"proj_bank{i}", [C, 512], F32)) for i in range(4)]
        s_h = [sem(f"h_loaded{p}") for p in range(NP)]
        s_w, s_bias, s_late = sem("w2_loaded"), sem("bias2_loaded"), sem("late2_loaded")
        s_kp, s_k = sem("key2_in_psum"), sem("key2_ready")
        s_vp, s_v = sem("value2_in_psum"), sem("value2_ready")

        with nc.Block() as block:
            @block.sync
            def _(sp):
                for p in range(NP):
                    t0, t1 = tiles_of(p)[0], tiles_of(p)[-1] + 1
                    sp.dma_start(hT[:, t0:t1, :, :].rearrange("c t h n -> c t (h n)"),
                                 hT_dram[t0:t1].rearrange("t c n -> c t n")).then_inc(s_h[p], 16)

            @block.scalar
            def _(act):
                act.dma_start(Wk_sb[:, :, :], Wk.rearrange("(k c) n -> c k n", c=C)).then_inc(s_w, 16)
                act.dma_start(Wv_sb[:, :, :], Wv.rearrange("(k c) n -> c k n", c=C)).then_inc(s_w, 16)
                with nc.allow_non_contiguous_dma("small bias columns"):
                    act.dma_start(bk_sb[:, :], bk.rearrange("(h c) -> c h", c=C)).then_inc(s_bias, 16)
                    act.dma_start(L["bq"][:, :], bq.rearrange("(h c) -> c h", c=C)).then_inc(s_late, 16)
                act.dma_start(bv_sb[:, :], bv.partition_broadcast(TP)).then_inc(s_bias, 16)
                act.dma_start(L["Wq"][:, :, :], Wq.rearrange("(k c) n -> c k n", c=C)).then_inc(s_late, 16)
                act.dma_start(L["Ws"][:, :, :], Ws.rearrange("(k c) n -> c k n", c=C)).then_inc(s_late, 16)
                act.wait_ge(s_bias, 32)
                for n in range(H2 * NP):
                    h, (a, b) = n % H2, PIECES[n // H2]
                    act.wait_ge(s_kp, n + 1)
                    act.activation(KT[:, h, a:b], bank[n % 2][:, 0:b - a], ACT.Identity,
                                   bias=bk_sb[:, h:h + 1]).then_inc(s_k, 1)
                act.wait_ge(s_late, 48)

            @block.vector
            def _(dve):
                dve.wait_ge(s_bias, 32)
                for t in range(NT):
                    dve.wait_ge(s_vp, t + 1)
                    dve.tensor_tensor(V[:, t, :], bank[2 + t % 2][0:TP, 0:H2 * C], bv_sb[:, :], ALU.add).then_inc(s_v, 1)

            @block.tensor
            def _(pe):
                pe.wait_ge(s_w, 32)
                n = 0
                for p, (a, b) in enumerate(PIECES):
                    pe.wait_ge(s_h[p], 16)
                    t0, t1 = tiles_of(p)[0], tiles_of(p)[-1] + 1
                    for h in range(H2):
                        wait(pe, s_k, n - 1)
                        for k in range(H1):
                            last = pe.matmul(bank[n % 2][:, 0:b - a], Wk_sb[:, k, h * C:(h + 1) * C],
                                             hT[:, t0:t1, k, :], start=k == 0, stop=k == H1 - 1)
                        last.then_inc(s_kp, 1)
                        n += 1
                    for t in tiles_of(p):
                        wait(pe, s_v, t - 1)
                        for k in range(H1):
                            last = pe.matmul(bank[2 + t % 2][0:TP, 0:H2 * C], hT[:, t, k, :], Wv_sb[:, k, :],
                                             start=k == 0, stop=k == H1 - 1)
                        last.then_inc(s_vp, 1)


def attention(nc, layer, H, KC, L, mask_dram, ident, hT_dram=None, xres=None, y=None, stats=None):
    featT, KT, V, Wq, Ws, bq = (L[n] for n in ("featT", "KT", "V", "Wq", "Ws", "bq"))
    W = H * C if layer == 1 else C
    LA = 4
    with ExitStack() as ctx:
        def sb(name, shape, dt=F32):
            return ctx.enter_context(nc.sbuf_tensor(f"{name}_l{layer}", shape, dt))

        def bank(name):
            return ctx.enter_context(nc.psum_tensor(f"{name}_l{layer}", [C, 512], F32))

        def sem(name):
            return ctx.enter_context(nc.semaphore(f"{name}_l{layer}"))

        QT = sb("QT", [C, H, TP])
        bq_s = sb("bq_scaled", [C, H])
        mask = sb("mask", [TP, N])
        prob = sb("prob", [TP, 2, N])
        probT = sb("probT", [TP, NP, PW])
        feat_now = sb("feat_now", [C, KC, TP])
        skip = sb("skip", [TP, W])
        rows = sb("rows", [TP, W])
        rowsT = sb("rowsT", [C, H * TP])
        piece_max = sb("piece_max", [TP, 2, NP])
        neg_max = sb("neg_max", [TP, 2])
        total = sb("total", [TP, 2])
        denom, inv, weight = sb("denom", [TP, 1]), sb("inv", [TP, 1]), sb("weight", [TP, 1])

        S = [bank(f"score{i}") for i in range(3)]
        T = [bank(f"transposed{i}") for i in range(2)]
        O, B_q, B_skip = bank("output"), bank("query"), bank("skip_rows")

        s_mask = [sem("mask_a"), sem("mask_b")]
        s_feat = sem("feat_ready")
        s_bq = sem("query_bias_ready")
        s_qp, s_q = sem("query_in_psum"), sem("query_ready")
        s_score, s_seen, s_masked = sem("score_ready"), sem("score_seen"), sem("score_masked")
        s_max, s_exp = sem("max_ready"), sem("exp_ready")
        s_tp = [sem("transposed_for_act"), sem("transposed_for_dve")]
        s_t = [sem("probT_by_act"), sem("probT_by_dve")]
        s_pv = sem("values_summed")
        s_out = sem("rows_ready")
        s_sp, s_skip = sem("skip_in_psum"), sem("skip_ready")
        s_rp, s_r, s_stored = sem("rowsT_in_psum"), sem("rowsT_ready"), sem("rowsT_stored")
        s_w0, s_w1, s_w2, s_half = sem("denom_ready"), sem("inverse_ready"), sem("weight_ready"), sem("half_sum_ready")
        per = (NP - NP // 2, NP // 2)

        def over_tiles(eng, body):
            body(0)
            with eng.Fori(1, NT - 1) as t:
                body(t)
            body(NT - 1)

        def is_last(t):
            return isinstance(t, int) and t == NT - 1

        def is_first(t):
            return isinstance(t, int) and t == 0

        with nc.Block() as block:
            @block.sync
            def _(sp):
                def load_mask(t, half):
                    a, b = ((0, PIECES[LA][0]), (PIECES[LA][0], N))[half]
                    for r0, r1 in ROW_SPLIT:
                        sp.dma_start(mask[r0:r1, a:b], mask_dram[bass.ds(t * TP + r0, r1 - r0), a:b]
                                     ).then_inc(s_mask[half], 16)

                def store_rowsT(t):
                    sp.wait_ge(s_r, t + 1)
                    sp.dma_start(hT_dram[bass.ds(t, 1)].rearrange("a p n -> (a p) n"), rowsT[:, :]).then_inc(s_stored, 16)

                def tile(t):
                    if not is_last(t):
                        for half in range(2):
                            sp.wait_ge(s_masked, NP * (H * t + H - 1) + (LA, NP)[half])
                            load_mask(t + 1, half)
                    if layer == 1:
                        store_rowsT(t)

                load_mask(0, 0)
                load_mask(0, 1)
                over_tiles(sp, tile)
                if layer == 1:
                    sp.wait_ge(s_stored, 16 * NT)

            @block.gpsimd
            def _(pool):
                def tile(t):
                    wait(pool, s_sp, t)
                    pool.tensor_copy(feat_now[:, :, :].rearrange("c k n -> c (k n)"),
                                     featT[:, bass.ds(t, 1), :, :].rearrange("c a k n -> c (a k n)")).then_inc(s_feat, 1)

                over_tiles(pool, tile)

            @block.scalar
            def _(act):
                def query(n, h):
                    act.wait_ge(s_qp, n + 1)
                    act.activation(QT[:, h, :], B_q[:, 0:TP], ACT.Identity, bias=bq_s[:, h:h + 1],
                                   scale=SCALE).then_inc(s_q, 1)

                def tile(t):
                    for h in range(H):
                        s = t * H + h
                        act.wait_ge(s_max, s + 1)
                        act.activation(prob[:, h % 2, :], prob[:, h % 2, :], ACT.Exp, bias=neg_max[:, h % 2:h % 2 + 1],
                                       accum_out=total[:, h % 2:h % 2 + 1]).then_inc(s_exp, 1)
                        if not is_last(t):
                            query(H + s, h)
                        for p in range(0, NP, 2):
                            a, b = PIECES[p]
                            act.wait_ge(s_tp[0], per[0] * s + p // 2 + 1)
                            wait(act, s_pv, NP * (s - 1) + p + 1)
                            act.copy(probT[:, p, 0:b - a], T[0][0:TP, 0:b - a]).then_inc(s_t[0], 1)

                act.mul(bq_s[:, :], bq[:, :], SCALE).then_inc(s_bq, 1)
                act.wait_ge(s_bq, 1)
                for h in range(H):
                    query(h, h)
                over_tiles(act, tile)

            @block.vector
            def _(dve):
                def masked_scores(s, h, first_of_tile, t):
                    wait(dve, s_max, s - 1)
                    for p, (a, b) in enumerate(PIECES):
                        if first_of_tile and p in (0, LA):
                            dve.wait_ge(s_mask[p // LA], 16 * len(ROW_SPLIT) * (t + 1))
                        dve.wait_ge(s_score, NP * s + p + 1).then_inc(s_seen, 1)
                        dve.tensor_tensor_reduce(out=prob[:, h % 2, a:b], in0=S[p % 3][0:TP, 0:b - a], in1=mask[:, a:b],
                                                 scale=1.0, scalar=-3.0e38, op0=ALU.add, op1=ALU.max,
                                                 accum_out=piece_max[:, h % 2, p:p + 1]).then_inc(s_masked, 1)
                    dve.wait_ge(s_masked, NP * (s + 1))
                    dve.tensor_reduce(neg_max[:, h % 2:h % 2 + 1], piece_max[:, h % 2, :], AX.X, ALU.max,
                                      negate=True).then_inc(s_max, 1)

                def rows_transposed(t):
                    dve.wait_ge(s_rp, t + 1)
                    wait(dve, s_stored, 16 * t)
                    dve.tensor_scalar(rowsT[:, :], B_skip[:, 0:H * TP], 0.0, None, ALU.max).then_inc(s_r, 1)

                def tile(t):
                    for h in range(H):
                        s = t * H + h
                        if not (is_last(t) and h == H - 1):
                            masked_scores(s + 1, (h + 1) % H, h == H - 1, t + 1)
                        if layer == 1 and h == 0 and not is_first(t):
                            rows_transposed(t - 1)
                        for p in range(1, NP, 2):
                            a, b = PIECES[p]
                            dve.wait_ge(s_tp[1], per[1] * s + p // 2 + 1)
                            wait(dve, s_pv, NP * (s - 1) + p + 1)
                            dve.tensor_copy(probT[:, p, 0:b - a], T[1][0:TP, 0:b - a]).then_inc(s_t[1], 1)
                        if h == 0:
                            dve.wait_ge(s_sp, t + 1)
                            add = L["bs"][:, :] if layer == 1 else xres[:, bass.ds(t, 1), :].rearrange("p a c -> p (a c)")
                            dve.tensor_tensor(skip[:, :], B_skip[0:TP, 0:W], add, ALU.add).then_inc(s_skip, 1)
                        dve.wait_ge(s_exp, s + 1)
                        dve.tensor_scalar(denom[:, :], total[:, h % 2:h % 2 + 1], 1.0 if layer == 1 else float(H2),
                                          EPS_DENOM, ALU.mult, ALU.add).then_inc(s_w0, 1)
                        dve.wait_ge(s_w0, s + 1)
                        dve.reciprocal(inv[:, :], denom[:, :]).then_inc(s_w1, 1)
                        dve.wait_ge(s_w1, s + 1)
                        dve.scalar_tensor_tensor(weight[:, :], neg_max[:, h % 2:h % 2 + 1], NO_EDGE, inv[:, :],
                                                 ALU.is_lt, ALU.mult).then_inc(s_w2, 1)
                        dve.wait_ge(s_w2, s + 1)
                        dve.wait_ge(s_skip, t + 1)
                        dve.wait_ge(s_pv, NP * (s + 1))
                        o = O[0:TP, 0:C]
                        if layer == 1:
                            dve.scalar_tensor_tensor(rows[:, h * C:(h + 1) * C], o, weight[:, 0:1], skip[:, h * C:(h + 1) * C],
                                                     ALU.mult, ALU.add).then_inc(s_out, 1)
                        elif h == 0:
                            dve.scalar_tensor_tensor(rows[:, :], o, weight[:, 0:1], skip[:, :],
                                                     ALU.mult, ALU.add).then_inc(s_out, 1)
                        else:
                            dve.wait_ge(s_out, s)
                            yt = y[:, bass.ds(t, 1), :].rearrange("p a c -> p (a c)")
                            dve.scalar_tensor_tensor(yt, o, weight[:, 0:1], rows[:, :], ALU.mult, ALU.add).then_inc(s_out, 1)
                            dve.wait_ge(s_out, s + 1)
                            dve.bn_stats(stats[:, bass.ds(t, 1), :].rearrange("p a c -> p (a c)"), yt)

                masked_scores(0, 0, True, 0)
                over_tiles(dve, tile)
                if layer == 1:
                    rows_transposed(NT - 1)

            @block.tensor
            def _(pe):
                def query(n, t, h):
                    wait(pe, s_q, n)
                    for k in range(KC):
                        last = pe.matmul(B_q[:, 0:TP], Wq[:, k, h * C:(h + 1) * C],
                                         featT[:, bass.ds(t, 1), k, :].rearrange("c a n -> c (a n)"),
                                         start=k == 0, stop=k == KC - 1)
                    last.then_inc(s_qp, 1)

                def scores(s, h, pieces):
                    if pieces[0] == 0:
                        pe.wait_ge(s_q, s + 1)
                    for p in pieces:
                        a, b = PIECES[p]
                        back = (0, -2, -1)[p] if p < 3 else p - 2
                        wait(pe, s_masked, NP * s + back)
                        pe.matmul(S[p % 3][0:TP, 0:b - a], QT[:, h, :], KT[:, h, a:b],
                                  start=True, stop=True).then_inc(s_score, 1)

                def skip_product(t):
                    pe.wait_ge(s_feat, t + 1)
                    if layer == 1:
                        wait(pe, s_r, t)
                    else:
                        wait(pe, s_skip, t)
                    for k in range(KC):
                        last = pe.matmul(B_skip[0:TP, 0:W], feat_now[:, k, :], Ws[:, k, :], start=k == 0, stop=k == KC - 1)
                    last.then_inc(s_sp, 1)

                def rows_transposed(t):
                    pe.wait_ge(s_out, H * (t + 1))
                    for h in range(H):
                        last = pe.transpose(B_skip[:, h * TP:(h + 1) * TP], rows[:, h * C:(h + 1) * C], ident[0:TP, 0:TP])
                    last.then_inc(s_rp, 1)

                def transposes(s, p, h):
                    wait(pe, s_t[p % 2], per[p % 2] * s + p // 2)
                    for i, t in enumerate(tiles_of(p)):
                        last = pe.transpose(T[p % 2][0:TP, i * TP:(i + 1) * TP], prob[:, h % 2, t * TP:(t + 1) * TP],
                                            ident[0:TP, 0:TP])
                    last.then_inc(s_tp[p % 2], 1)

                def values(s, p, h):
                    pe.wait_ge(s_t[p % 2], per[p % 2] * s + p // 2 + 1)
                    if p == 0:
                        wait(pe, s_out, s)
                    for i, t in enumerate(tiles_of(p)):
                        last = pe.matmul(O[0:TP, 0:C], probT[:, p, i * TP:(i + 1) * TP],
                                         V[:, t, h * C:(h + 1) * C], start=t == 0, stop=t == NT - 1)
                    last.then_inc(s_pv, 1)

                def tile(t):
                    for h in range(H):
                        s = t * H + h
                        more = not (is_last(t) and h == H - 1)
                        if more:
                            scores(s + 1, (h + 1) % H, range(0, NP - 2))
                        if layer == 1 and h == 0 and not is_first(t):
                            rows_transposed(t - 1)
                        if not is_last(t):
                            query(H + s, t + 1, h)
                        pe.wait_ge(s_exp, s + 1)
                        transposes(s, 0, h)
                        if more:
                            scores(s + 1, (h + 1) % H, [NP - 2])
                        transposes(s, 1, h)
                        if more:
                            scores(s + 1, (h + 1) % H, [NP - 1])
                        for p in range(NP):
                            values(s, p, h)
                            if p + 2 < NP:
                                transposes(s, p + 2, h)
                            if p == 3 and h == 0:
                                skip_product(t)

                for h in range(H):
                    query(h, 0, h)
                scores(0, 0, range(NP))
                over_tiles(pe, tile)
                if layer == 1:
                    rows_transposed(NT - 1)


def layer_norm(nc, y, stats, out):
    with ExitStack() as ctx:
        moments = ctx.enter_context(nc.sbuf_tensor("moments", [TP, NT, 2], F32))
        dev = ctx.enter_context(nc.sbuf_tensor("dev", [TP, NT], F32))
        eps = ctx.enter_context(nc.sbuf_tensor("eps", [TP, 1], F32))
        s_eps, s_mom, s_dev, s_inv, s_y, s_outd = (ctx.enter_context(nc.semaphore(n)) for n in
                                             ("eps_ready", "moments_ready", "dev_ready", "inv_dev_ready", "y_ready", "out_stored"))
        with nc.Block() as block:
            @block.vector
            def _(dve):
                dve.memset(eps[:, :], EPS_NORM).then_inc(s_eps, 1)
                for t in range(NT):
                    dve.bn_aggr(moments[:, t, :], stats[:, t, :]).then_inc(s_mom, 1)
                dve.wait_ge(s_dev, 1)
                dve.reciprocal(dev[:, :], dev[:, :]).then_inc(s_inv, 1)
                dve.wait_ge(s_inv, 1)
                for t in range(NT):
                    dve.tensor_scalar(y[:, t, :], y[:, t, :], moments[:, t, 0:1], dev[:, t:t + 1],
                                      ALU.subtract, ALU.mult).then_inc(s_y, 1)

            @block.scalar
            def _(act):
                act.wait_ge(s_eps, 1)
                act.wait_ge(s_mom, NT)
                act.activation(dev[:, :], moments[:, :, 1], ACT.Sqrt, bias=eps[:, 0:1]).then_inc(s_dev, 1)

            @block.sync
            def _(sp):
                sp.wait_ge(s_y, NT)
                sp.dma_start(out.rearrange("(t p) c -> p t c", p=TP), y[:, :, :]).then_inc(s_outd, 16)
                sp.wait_ge(s_outd, 16)


_INS = ["x", "src", "dst"] + ["L0_gnn_" + a + b + n for n in "12" for a, b in
                              (("W", "q"), ("b", "q"), ("W", "k"), ("b", "k"), ("W", "v"), ("b", "v"), ("W", "s"), ("b", "s"))]


def kernel(**inputs):
    import numpy as _np
    import concourse.bacc as _bacc
    from concourse import mybir as _mybir
    from concourse.bass_utils import run_bass_kernel_spmd as _run

    nc = _bacc.Bacc("TRN2", target_bir_lowering=False, num_devices=1)
    arrays, args = {}, []
    for name in _INS:
        a = _np.ascontiguousarray(inputs[name])
        arrays[f"in_{name}"] = a
        args.append(nc.dram_tensor(f"in_{name}", a.shape, _mybir.dt.from_np(a.dtype), kind="ExternalInput").ap())
    args.append(nc.dram_tensor("out", (N, C), F32, kind="ExternalOutput").ap())
    build(nc, *args)
    r = _run(nc, [arrays], core_ids=[0])
    return r.results[0]["out"]
```

```python
from contextlib import ExitStack

import concourse.bass as bass
import concourse.mybir as mybir

F32 = mybir.dt.float32
F16 = mybir.dt.float16
BF16 = mybir.dt.bfloat16
I32 = mybir.dt.int32
ALU = mybir.AluOpType
ACT = mybir.ActivationFunctionType
AX = mybir.AxisListType
RMAX = bass.bass_isa.ReduceOp.max

N = 3125
TP = 125
NT = N // TP
C = 128
H1, H2 = 4, 2
E = 103125
CE = 125
NCH = E // CE
CG = 11
CP = NCH // CG
PT = 4
PW = PT * TP
PIECES = [(a, min(a + PW, N)) for a in range(0, N, PW)]
NP = len(PIECES)
EXP_PARTS = ((0, 1), (2, 3), (4, 5, 6))
LEAD = 5
ROW_SPLIT = ((0, 112), (112, TP))
SA = 5
SB = N // SA
NB = 2
WR = NB * TP
WD = WR // SA
NW = -(-N // (2 * WD)) * 2
HB = -(-SB // 2)
KF = 15
KF0, KF1 = 9, 5
ROWS_BY_ACT = ((1, 2), (3, 4), (9, 10), (11, 12), (13, 14))
MASKS_AFTER = (8, 11)
LOGS_BEFORE = (2, 3)
NEXT_AFTER = 8
RING = 5
PAD = -1.0
BIG = 2.0 ** 100
SCALE = float(C) ** -0.5
TINY = 1e-30
NO_EDGE = 1e28
P_UP = 2.0 ** 14
V_UP = 2.0 ** 12
EXPONENT = 0x7F800000
INVERSE = 254 << 23
EPS_DENOM = 1e-16
EPS_NORM = 1e-5


def blocks_of(k):
    return [v for v, has in enumerate((k < KF0, k >= KF1)) if has]


def group_of(k):
    return next((g for g, chunks in enumerate(ROWS_BY_ACT) if k in chunks), None)


def wait(eng, sem, value):
    if not (isinstance(value, int) and value <= 0):
        eng.wait_ge(sem, value)


def tiles_of(p):
    return range(PIECES[p][0] // TP, PIECES[p][1] // TP)


def build(nc, x, src, dst, Wq1, bq1, Wk1, bk1, Wv1, bv1, Ws1, bs1,
          Wq2, bq2, Wk2, bk2, Wv2, bv2, Ws2, bs2, out):
    mask_dram = nc.dram_tensor("mask_scratch", (NW * WD, N), F32, kind="Internal").ap()
    hT_dram = nc.dram_tensor("hT_scratch", (NT, C, H1 * TP), F32, kind="Internal").ap()

    with ExitStack() as ctx:
        def sb(name, shape, dt=F32):
            return ctx.enter_context(nc.sbuf_tensor(name, shape, dt))

        ident = sb("ident", [C, C])
        h_max = sb("h_max", [C, H1, NT, 1])
        xres = sb("xres", [TP, NT, C])
        with ExitStack() as lay:
            def sb1(name, shape, dt=F32):
                return lay.enter_context(nc.sbuf_tensor(name, shape, dt))

            layer1 = {
                "featT": sb1("xT", [C, NT, 1, TP]),
                "KT": sb1("KT1", [C, H1, 2, N], F16),
                "V": sb1("V1", [TP, NT, H1, 2, C], F16),
                "v_back": sb1("v_back1", [C, H1 * C]),
                "Wq": sb1("Wq1_sb", [C, 1, H1 * C]),
                "Ws": sb1("Ws1_sb", [C, 1, H1 * C]),
                "bq": sb1("bq1_sb", [C, H1]),
                "bs": sb1("bs1_sb", [TP, H1 * C]),
            }
            mask_and_projections(nc, x, src, dst, Wk1, bk1, Wv1, bv1, Wq1, bq1, Ws1, bs1, bs2,
                                 ident, xres, layer1, mask_dram)
            attention(nc, 1, H1, 1, layer1, mask_dram, ident, hT_dram=hT_dram, h_max=h_max)
        with ExitStack() as lay:
            def sb2(name, shape, dt=F32):
                return lay.enter_context(nc.sbuf_tensor(name, shape, dt))

            layer2 = {
                "featT": sb2("hT", [C, NT, H1, TP]),
                "KT": sb2("KT2", [C, H2, 2, N], F16),
                "V": sb2("V2", [TP, NT, H2, 2, C], F16),
                "v_back": sb2("v_back2", [C, H2 * C]),
                "Wq": sb2("Wq2_sb", [C, H1, H2 * C]),
                "Ws": sb2("Ws2_sb", [C, H1, C]),
                "bq": sb2("bq2_sb", [C, H2]),
            }
            y = sb2("y", [TP, NT, C])
            stats = sb2("stats", [TP, NT, 6])
            projections2(nc, Wk2, bk2, Wv2, bv2, Wq2, bq2, Ws2, layer2, hT_dram, h_max, ident)
            attention(nc, 2, H2, H1, layer2, mask_dram, ident, xres=xres, y=y, stats=stats)
            layer_norm(nc, y, stats, out)


class Scales:

    def __init__(self, nc, sb, sem, layer, H, KC, W, v_row, bias_cols, v_back, abs_w, up, bank, ident):
        self.nc, self.H, self.KC, self.W = nc, H, KC, W
        self.v_row, self.cols = v_row, bias_cols
        self.v_back, self.abs_w, self.bank, self.ident = v_back, abs_w, bank, ident
        self.top = sb(f"feature_max{layer}", [C, KC])
        self.top_b = sb(f"feature_max_b{layer}", [C, KC, C])
        self.abs_rows = sb(f"bias_rows{layer}", [C, 3, H * C])
        self.up = up
        names = ("abs_weights", "feature_bounds", "bounds_summed", "ratio", "root", "scales", "scale_columns", "scaled")
        (self.s_abs, self.s_top, self.s_bound, self.s_ratio, self.s_root, self.s_up, self.s_colp, self.s_scaled) = (
            sem(f"{n}_ready{layer}") for n in names)

    def magnitudes(self, act):
        for i in range(3):
            act.activation(self.abs_w[:, i, :, :], self.W[i][:, :, :], ACT.Abs).then_inc(self.s_abs, 1)
            act.activation(self.abs_rows[:, i, :], self.v_row[:, :] if i == 2 else self.abs_rows[:, i, :], ACT.Abs).then_inc(self.s_abs, 1)

    def root(self, act):
        act.wait_ge(self.s_ratio, 1)
        act.activation(self.up[:, 0, :], self.up[:, 0, :], ACT.Sqrt).then_inc(self.s_root, 1)

    def bounds(self, pe):
        pe.wait_ge(self.s_abs, 6)
        pe.wait_ge(self.s_top, 1)
        for i in range(3):
            for k in range(self.KC):
                last = pe.matmul(self.bank[i][:, 0:self.H * C], self.top_b[:, k, :], self.abs_w[:, i, k, :],
                                 start=k == 0, stop=k == self.KC - 1)
            last.then_inc(self.s_bound, 1)

    def columns(self, pe):
        pe.wait_ge(self.s_up, 1)
        for i in range(2):
            for h in range(self.H):
                n = i * self.H + h
                last = pe.matmul(self.bank[4][:, n:n + 1], self.up[0:1, i, h * C:(h + 1) * C], self.ident[0:1, 0:1],
                                 start=True, stop=True)
        last.then_inc(self.s_colp, 1)

    def largest(self, dve, link, features):
        link(dve.tensor_reduce(self.top[:, :], features, AX.XY, ALU.max, apply_absolute_value=True))
        dve.tensor_copy(self.top_b[:, :, :], self.top[:, :].unsqueeze(2).broadcast_to([C, self.KC, C])
                        ).then_inc(self.s_top, 1)

    def scale(self, dve, link):
        up, bound, H = self.up, self.abs_rows, self.H

        def power(to, of):
            link(dve.tensor_scalar(to.bitcast(I32), of.bitcast(I32), EXPONENT, None, ALU.bitwise_and))

        def inverse(to, of, sem=None):
            link(dve.tensor_scalar(to.bitcast(I32), of.bitcast(I32), -1, INVERSE, ALU.mult, ALU.add), sem)

        for i in range(3):
            dve.wait_ge(self.s_bound, i + 1)
            ins = dve.scalar_tensor_tensor(bound[:, i, :], self.bank[i][:, 0:H * C], TINY, bound[:, i, :], ALU.max, ALU.add)
        link(ins)
        power(up[:, 0, :], bound[:, 0, :])
        inverse(up[:, 0, :], up[:, 0, :])
        dve.tensor_tensor(up[:, 0, :], bound[:, 1, :], up[:, 0, :], ALU.mult).then_inc(self.s_ratio, 1)
        power(self.v_back[:, :], bound[:, 2, :])
        inverse(up[:, 2, :], self.v_back[:, :])
        dve.tensor_scalar(self.v_back[:, :], self.v_back[:, :], 1.0 / (V_UP * P_UP), None, ALU.mult)
        link(dve.tensor_scalar(up[:, 2, :], up[:, 2, :], V_UP, None, ALU.mult))
        dve.wait_ge(self.s_root, 1)
        power(up[:, 0, :], up[:, 0, :])
        inverse(up[:, 1, :], up[:, 0, :], self.s_up)
        for i in (0, 2, 1):
            w = self.W[i]
            factor = up[:, i, :].unsqueeze(1).broadcast_to([C, self.KC, H * C])
            dve.tensor_tensor(w[:, :, :], w[:, :, :], factor, ALU.mult).then_inc(self.s_scaled, 1)
        dve.tensor_tensor(self.v_row[:, :], self.v_row[:, :], up[:, 2, :], ALU.mult).then_inc(self.s_scaled, 1)
        dve.wait_ge(self.s_colp, 1)
        for i in range(2):
            b = self.cols[i]
            dve.tensor_tensor(b[:, :], b[:, :], self.bank[4][:, i * H:(i + 1) * H], ALU.mult).then_inc(self.s_scaled, 1)
        self.wait_scaled(dve)

    def wait_weights(self, eng):
        eng.wait_ge(self.s_scaled, 2)

    def wait_scaled(self, eng):
        eng.wait_ge(self.s_scaled, 6)


def mask_and_projections(nc, x, src, dst, Wk, bk, Wv, bv, Wq, bq, Ws, bs, bs2,
                         ident, xres, L, mask_dram):
    xT, KT, V = L["featT"], L["KT"], L["V"]
    with ExitStack() as ctx:
        def sb(name, shape, dt=F32):
            return ctx.enter_context(nc.sbuf_tensor(name, shape, dt))

        def sem(name):
            return ctx.enter_context(nc.semaphore(name))

        Wk_sb, Wv_sb = sb("Wk1_sb", [C, 1, H1 * C]), sb("Wv1_sb", [C, 1, H1 * C])
        bk_sb, bv_sb = sb("bk1_sb", [C, H1]), sb("bv1_sb", [C, H1 * C])
        work = sb("work", [C, 5 * 512])
        abs_w = work[:, 0:3 * H1 * C].rearrange("c (i k n) -> c i k n", i=3, k=1)
        k_now = work[:, 3 * H1 * C:].rearrange("c (i n) -> c i n", i=2)
        v_now = sb("v_now", [TP, 2, H1, C])
        bs2_sb = sb("bs2_sb", [TP, C])
        ends_i = sb("ends_i", [CP, 2, CG * CE], I32)
        ends_f = ends_i[:, :, :].bitcast(F32)
        digit = sb("digit", [CE, NCH])
        at_least = v_now[:, :, :, :].rearrange("p i h c -> p (i h c)")[:, 0:NCH]
        row_of, col_of = sb("row_of", [CE, NCH + KF]), sb("col_of", [CE, NCH + KF])
        dstE, srcE = row_of[:, 0:NCH], col_of[:, 0:NCH]
        rows, cols = sb("rows", [CE, WR], F16), sb("cols", [CE, 2 * HB], F16)
        base = sb("base", [CE, NW])
        hot = sb("hot", [C, RING * 2 * HB], BF16)
        col_hot = hot[0:CE, :].rearrange("e (r n) -> e r n", r=RING)
        up = hot[:, 0:2 * 3 * H1 * C].bitcast(F32).rearrange("c (i n) -> c i n", i=3)
        zeros = sb("zeros", [1, HB], BF16)
        tiny = sb("tiny", [TP, 1])
        log = work[0:TP, 0:NB * 2 * HB].rearrange("p (v b) -> p v b", v=NB)
        row_buffer = work[0:CE, NB * 2 * HB:5 * 512].bitcast(BF16)
        row_pair = row_buffer[:, 0:2 * WR].rearrange("e (r n) -> e r n", r=2)
        win = sb("win", [CP, NW, CG])
        chunk_id = sb("chunk_id", [CP, CG])
        dmin, dmax = sb("dmin", [CP, CG]), sb("dmax", [CP, CG])
        below, touch = (sb(n, [CP, NW, CG]) for n in ("below", "touch"))
        span, span_all = sb("span", [CP, 4, NW]), sb("span_all", [CP, 4, NW])
        excess = sb("excess", [1, 3, NW])
        minus_rel, row_diff = sb("minus_rel", [CE, 2, KF]), sb("row_diff", [CE, 3, max(map(len, ROWS_BY_ACT)) * TP], BF16)
        one = sb("one", [CE, 1])
        first_c, steps_f, ends_cum, zero_row = (sb(n, [1, NW]) for n in ("first_c", "steps_f", "ends_cum", "zero_row"))
        end_c = sb("end_c", [1, NW])
        steps_i = sb("steps_i", [1, NW], I32)
        starts_f, offs_f = sb("starts_f", [1, NW]), sb("offs_f", [1, NW])
        table = sb("table", [1, 3, NW], I32)
        first_i = sb("first_i", [1, NW], I32)
        most, few = sb("most", [1, 1]), sb("few", [1, 1], I32)

        banks = ctx.enter_context(nc.psum_tensor("mask_banks", [C, 8, 512], F32))
        bank = [banks[:, i, :] for i in range(5)]

        def counts(u, v):
            i = 2 * NB * u + 2 * v
            return banks[0:TP, i:i + 2, 0:HB]

        s_ends = [sem("dst_loaded"), sem("src_loaded")]
        s_x, s_wk, s_bias, s_late = (sem(n) for n in ("x_loaded", "weights_loaded", "bias_loaded", "late_loaded"))
        s_ident0, s_ident, s_const = sem("ident_zeroed"), sem("ident_ready"), sem("const_ready")
        s_dve = sem("dve_chain")
        s_xtp, s_xt = sem("xT_in_psum"), sem("xT_ready")
        s_kp, s_k = sem("key_in_psum"), sem("key_ready")
        s_vp, s_v = sem("value_in_psum"), sem("value_ready")
        s_ep, s_e = sem("ends_in_psum"), sem("ends_ready")
        s_span, s_all = sem("span_ready"), sem("span_reduced")
        s_table = sem("table_ready")
        s_hot, s_hot_free = sem("hot_ready"), sem("hot_free")
        s_rel, s_diff, s_row_act = sem("relative_rows_ready"), sem("row_difference_ready"), sem("rows_by_act_ready")
        s_cnt = sem("count_in_psum")
        s_log, s_masked = sem("logarithm_ready"), sem("mask_ready")
        s_stored = [sem("mask_stored_even"), sem("mask_stored_odd")]
        s_cols = sem("columns_ready")
        s_klo, s_vhi, s_vlo = sem("key_lo_ready"), sem("value_hi_ready"), sem("value_lo_ready")
        s_rows, s_digit, s_list = sem("bias_rows_loaded"), sem("digit_chain"), sem("edge_list_converted")

        scales = Scales(nc, sb, sem, 1, H1, 1, (Wk_sb, L["Wq"], Wv_sb), bv_sb,
                        (bk_sb, L["bq"]), L["v_back"], abs_w, up, bank, ident)

        STORED = 16 * len(ROW_SPLIT)

        def row_hot(k, v=None):
            start = sum(len(blocks_of(q)) for q in range(k)) * TP
            if v is None:
                return row_buffer[:, start:start + len(blocks_of(k)) * TP]
            start += blocks_of(k).index(v) * TP
            return row_buffer[:, start:start + TP]

        def rows_cut(k):
            return slice(blocks_of(k)[0] * TP, (blocks_of(k)[-1] + 1) * TP)

        def ends_in(eng, which, dram):
            eng.dma_start(ends_i[:, which, :], dram.rearrange("(p n) -> p n", p=CP)).then_inc(s_ends[which], 16)

        XG = 4
        x_groups = [range(a, min(a + XG, NT)) for a in range(0, NT, XG)]
        EG = 6
        e_groups = [(w, g, min(g + EG, CG)) for w in range(2) for g in range(0, CG, EG)]
        KB, VB, EB = (0, 1), (2, 3), (0, 1)

        with nc.Block() as block:
            @block.sync
            def _(sp):
                ends_in(sp, 0, dst)
                sp.dma_start(xres[:, :, :], x.rearrange("(t p) c -> p t c", p=TP)).then_inc(s_x, 16)
                ends_in(sp, 1, src)
                blocks = mask_dram.rearrange("(w j) (a b) -> w (j a) b", j=TP // SA, a=SA)
                with sp.Fori(0, NW) as w:
                    for v in range(NB):
                        sp.wait_ge(s_masked, NB * (w + 2) + v + 1)
                        for r0, r1 in ROW_SPLIT:
                            sp.dma_start(blocks[bass.ds(NB * w + v, 1), r0:r1, :].rearrange("w p b -> (w p) b"),
                                         log[r0:r1, v, 0:SB]).then_inc(s_stored[v], 16)
                for v in range(NB):
                    sp.wait_ge(s_stored[v], STORED * NW)

            @block.scalar
            def _(act):
                act.dma_start(Wk_sb[:, 0, :], Wk).then_inc(s_wk, 16)
                act.dma_start(L["Wq"][:, 0, :], Wq).then_inc(s_wk, 16)
                act.dma_start(Wv_sb[:, 0, :], Wv).then_inc(s_wk, 16)
                for i, b in enumerate((bk, bq)):
                    act.dma_start(scales.abs_rows[:, i, :], b.partition_broadcast(C)).then_inc(s_rows, 16)
                act.dma_start(bv_sb[:, :], bv.partition_broadcast(C)).then_inc(s_rows, 16)
                with nc.allow_non_contiguous_dma("small bias columns"):
                    act.dma_start(bk_sb[:, :], bk.rearrange("(h c) -> c h", c=C)).then_inc(s_bias, 16)
                    act.dma_start(L["bq"][:, :], bq.rearrange("(h c) -> c h", c=C)).then_inc(s_bias, 16)
                act.dma_start(bs2_sb[:, :], bs2.partition_broadcast(TP)).then_inc(s_bias, 16)
                act.dma_start(L["bs"][:, :], bs.partition_broadcast(TP)).then_inc(s_late, 16)
                act.dma_start(L["Ws"][:, 0, :], Ws).then_inc(s_late, 16)
                for n, g in enumerate(x_groups):
                    act.wait_ge(s_xtp, n + 1)
                    act.copy(xT[:, g[0]:g[-1] + 1, 0, :].rearrange("c t n -> c (t n)"),
                             bank[EB[n % 2]][:, 0:len(g) * TP]).then_inc(s_xt, 1)
                act.wait_ge(s_wk, 48)
                act.wait_ge(s_rows, 48)
                scales.magnitudes(act)
                scales.root(act)
                scales.wait_scaled(act)
                for n in range(H1 * NP):
                    h, (a, b) = n // NP, PIECES[n % NP]
                    act.wait_ge(s_kp, n + 1)
                    wait(act, s_klo, n - 1)
                    for to in (k_now[:, n % 2, 0:b - a], KT[:, h, 0, a:b]):
                        act.activation(to, bank[KB[n % 2]][:, 0:b - a], ACT.Identity, bias=bk_sb[:, h:h + 1]).then_inc(s_k, 1)
                    if n < NT:
                        act.wait_ge(s_v, n + 1)
                        act.copy(V[:, n, :, 0, :], v_now[:, n % 2, :, :]).then_inc(s_vhi, 1)
                act.wait_ge(s_late, 32)
                act.wait_ge(s_const, 7)
                def logarithm(w, u, v):
                    if v == 0:
                        act.wait_ge(s_cnt, w + 1)
                    wait(act, s_stored[v], STORED * w)
                    act.activation(log[:, v, :].rearrange("p (a b) -> p a b", a=2), counts(u, v), ACT.Ln,
                                   bias=tiny[:, 0:1], scale=1.0 / BIG).then_inc(s_log, 1)

                NA = len(ROWS_BY_ACT)

                def width(n):
                    return sum(len(blocks_of(k)) for k in ROWS_BY_ACT[n]) * TP

                def row_difference(w, u, n):
                    if n == 0:
                        act.wait_ge(s_rel, w + 1)
                    wait(act, s_row_act, NA * (w + 1) + max(n - 2, 0))
                    start = 0
                    for k in ROWS_BY_ACT[n]:
                        cut = rows_cut(k)
                        end = start + cut.stop - cut.start
                        last = act.activation(row_diff[:, n % 3, start:end], rows[:, cut], ACT.Square, bias=minus_rel[:, u, k:k + 1])
                        start = end
                    last.then_inc(s_diff, 1)

                def make_rows(w, u, n):
                    act.wait_ge(s_diff, NA * w + n + 1)
                    k0, k1 = ROWS_BY_ACT[n][0], ROWS_BY_ACT[n][-1]
                    wait(act, s_hot_free, KF * (w - 1) + k1 + 1 + RING)
                    start = sum(len(blocks_of(q)) for q in range(k0)) * TP
                    act.activation(row_buffer[:, start:start + width(n)], row_diff[:, n % 3, 0:width(n)], ACT.Relu,
                                   bias=one[:, 0:1], scale=-1.0).then_inc(s_row_act, 1)

                def first_rows(w, u):
                    row_difference(w, u, 0)
                    for n in range(LOGS_BEFORE[0]):
                        if n + 1 < NA:
                            row_difference(w, u, n + 1)
                        make_rows(w, u, n)

                def other_rows(w, u, last=None):
                    for n in range(LOGS_BEFORE[0], NA):
                        if last is not None and n in LOGS_BEFORE:
                            logarithm(last, 1 - u, LOGS_BEFORE.index(n))
                        if n + 1 < NA:
                            row_difference(w, u, n + 1)
                        make_rows(w, u, n)

                act.wait_ge(s_table, 2)
                is_few = act.value_load(few[0:1, 0:1], min_val=0, max_val=1)
                with act.If(is_few > 0):
                    first_rows(0, 0)
                    other_rows(0, 0)
                    first_rows(1, 1)
                    with act.Fori(0, NW // 2 - 1) as i:
                        for u in (1, 0):
                            w = 2 * i + 2 - u
                            other_rows(w, u, w - 1)
                            first_rows(w + 1, 1 - u)
                    other_rows(NW - 1, 1, NW - 2)
                    for v in range(NB):
                        logarithm(NW - 1, 1, v)
                with act.Else():
                    with act.Fori(0, NW // 2) as i:
                        for u in range(2):
                            for v in range(NB):
                                logarithm(2 * i + u, u, v)

            @block.gpsimd
            def _(pool):
                pool.memset(ident[:, :], 0.0).then_inc(s_ident0, 1)
                pool.wait_ge(s_ident0, 1)
                pool.affine_select(out=ident[:, :], in_=ident[:, :], compare_op=ALU.not_equal, fill=1.0, base=0,
                                   pattern=[[-1, C]], channel_multiplier=1).then_inc(s_ident, 1)
                pool.iota(win[:, :, :], [[WD, NW], [0, CG]], base=0, channel_multiplier=0,
                          allow_small_or_imprecise_dtypes=True).then_inc(s_const, 1)
                pool.iota(chunk_id[:, :], [[1, CG]], base=0, channel_multiplier=CG,
                          allow_small_or_imprecise_dtypes=True).then_inc(s_const, 1)
                pool.iota(base[:, :], [[-WR, NW]], base=0, channel_multiplier=0,
                          allow_small_or_imprecise_dtypes=True).then_inc(s_const, 1)
                pool.memset(tiny[:, :], TINY).then_inc(s_const, 1)
                pool.memset(one[:, :], 1.0).then_inc(s_const, 1)
                pool.iota(rows[:, :], [[1, WR]], base=0, channel_multiplier=0,
                          allow_small_or_imprecise_dtypes=True).then_inc(s_const, 1)
                pool.iota(cols[:, :], [[1, 2 * HB]], base=0, channel_multiplier=0,
                          allow_small_or_imprecise_dtypes=True).then_inc(s_const, 1)
                steps = [0]

                def link(ins):
                    steps[0] += 1
                    ins.then_inc(s_digit, 1)
                    pool.wait_ge(s_digit, steps[0])

                pool.wait_ge(s_e, len(e_groups))
                link(pool.tensor_scalar(digit[:, :], srcE, float(SB), None, ALU.is_ge))
                for a in range(2, SA):
                    link(pool.tensor_scalar(at_least[:, :], srcE, float(a * SB), None, ALU.is_ge))
                    link(pool.tensor_tensor(digit[:, :], digit[:, :], at_least[:, :], ALU.add))
                link(pool.tensor_scalar(dstE, dstE, float(SA), None, ALU.mult))
                pool.tensor_tensor(dstE, dstE, digit[:, :], ALU.add).then_inc(s_cols, 1)
                link(pool.tensor_scalar(at_least[:, :], digit[:, :], float(SB), None, ALU.mult))
                pool.tensor_tensor(srcE, srcE, at_least[:, :], ALU.subtract).then_inc(s_cols, 1)
                for t in range(NT):
                    pool.wait_ge(s_vhi, t + 1)
                    pool.tensor_tensor(V[:, t, :, 1, :], v_now[:, t % 2, :, :], V[:, t, :, 0, :], ALU.subtract).then_inc(s_vlo, 1)
                    if t == 16:
                        pool.wait_ge(s_span, 4)
                        pool.partition_all_reduce(span_all[:, :, :].rearrange("p a t -> p (a t)"),
                                                  span[:, :, :].rearrange("p a t -> p (a t)"), CP, RMAX).then_inc(s_all, 1)
                pool.wait_ge(s_bias, 48)
                pool.wait_ge(s_xtp, len(x_groups))
                pool.tensor_tensor(xres[:, :, :], xres[:, :, :],
                                   bs2_sb[:, :].unsqueeze(1).broadcast_to([TP, NT, C]), ALU.add).then_inc(s_const, 1)

            @block.vector
            def _(dve):
                chain = [0]

                def link(ins, sem=None):
                    chain[0] += sem is None
                    ins.then_inc(sem or s_dve, 1)
                    dve.wait_ge(sem or s_dve, chain[0] if sem is None else 1)

                dve.memset(zeros[:, :], 0.0).then_inc(s_hot_free, RING)
                dve.memset(row_of[:, NCH:NCH + KF], PAD).then_inc(s_row_act, len(ROWS_BY_ACT))
                dve.memset(col_of[:, NCH:NCH + KF], PAD)
                dve.memset(zero_row[:, :], 0.0).then_inc(s_masked, 2 * NB)
                def ends(which):
                    dve.wait_ge(s_ends[which], 16)
                    dve.tensor_copy(ends_f[:, which, :], ends_i[:, which, :]).then_inc(s_list, 1)
                    dve.wait_ge(s_list, which + 1)

                def ends_on_partitions(which):
                    for n, (of, g0, g1) in enumerate(e_groups):
                        if of == which:
                            dve.wait_ge(s_ep, n + 1)
                            to = (dstE, srcE)[which][:, :].rearrange("e (p g) -> e g p", g=CG)[:, g0:g1, :]
                            dve.tensor_copy(to, bank[EB[n % 2]][0:CE, 0:(g1 - g0) * CP].rearrange("e (g p) -> e g p", p=CP)
                                            ).then_inc(s_e, 1)

                ends(0)
                d = ends_f[:, 0, :].rearrange("p (g e) -> p g e", g=CG)
                dve.tensor_reduce(dmin[:, :], d, AX.X, ALU.min)
                link(dve.tensor_reduce(dmax[:, :], d, AX.X, ALU.max))
                ends_on_partitions(0)
                ends(1)
                dve.wait_ge(s_const, 2)
                lo = dmin[:, :].unsqueeze(1).broadcast_to([CP, NW, CG])
                hi = dmax[:, :].unsqueeze(1).broadcast_to([CP, NW, CG])
                ids = chunk_id[:, :].unsqueeze(1).broadcast_to([CP, NW, CG])
                link(dve.tensor_tensor(below[:, :, :], lo, win[:, :, :], ALU.subtract))
                link(dve.tensor_scalar(below[:, :, :], below[:, :, :], float(WD), None, ALU.is_lt))
                link(dve.tensor_tensor(touch[:, :, :], hi, win[:, :, :], ALU.subtract))
                link(dve.scalar_tensor_tensor(touch[:, :, :], touch[:, :, :], 0.0, below[:, :, :], ALU.is_ge, ALU.mult))
                ends_on_partitions(1)

                def spans(part):
                    of = below if part >= 2 else touch
                    if part >= 2:
                        end, has = ((lo, ALU.is_lt), (hi, ALU.is_ge))[part - 2]
                        link(dve.tensor_tensor(below[:, :, :], end, win[:, :, :], ALU.subtract))
                        link(dve.scalar_tensor_tensor(below[:, :, :], below[:, :, :], float(WD // NB), touch[:, :, :], has, ALU.mult))
                    if part in (0, 3):
                        link(dve.scalar_tensor_tensor(below[:, :, :], ids, -float(NCH), of[:, :, :], ALU.add, ALU.mult))
                        ins = dve.tensor_reduce(span[:, part, :], below[:, :, :], AX.X, ALU.min, negate=True)
                    else:
                        link(dve.scalar_tensor_tensor(below[:, :, :], ids, 1.0, of[:, :, :], ALU.add, ALU.mult))
                        ins = dve.tensor_reduce(span[:, part, :], below[:, :, :], AX.X, ALU.max)
                    ins.then_inc(s_span, 1)
                    dve.wait_ge(s_span, part + 1)

                for part in range(3):
                    spans(part)
                dve.wait_ge(s_xt, len(x_groups))
                scales.largest(dve, link, xT[:, :, :, :].rearrange("c t k n -> c k t n"))
                spans(3)
                dve.wait_ge(s_bias, 48)
                scales.scale(dve, link)
                def tables():
                    dve.wait_ge(s_all, 1)
                    link(dve.tensor_scalar(first_c[:, :], span_all[0:1, 0, :], -1.0, float(NCH), ALU.mult, ALU.add))
                    link(dve.tensor_scalar(first_c[:, :], first_c[:, :], float(NCH - 1), None, ALU.min))
                    link(dve.tensor_tensor(end_c[:, :], span_all[0:1, 1, :], first_c[:, :], ALU.subtract))
                    dve.tensor_copy(first_i[:, :], first_c[:, :]).then_inc(s_table, 1)
                    dve.tensor_scalar(excess[:, 0, :], end_c[:, :], -float(KF), None, ALU.add)
                    dve.scalar_tensor_tensor(excess[:, 1, :], span_all[0:1, 2, :], -float(KF0), first_c[:, :], ALU.add, ALU.subtract)
                    link(dve.tensor_scalar(excess[:, 2, :], first_c[:, :], -1.0, float(NCH - KF1), ALU.mult, ALU.add))
                    link(dve.scalar_tensor_tensor(excess[:, 2, :], excess[:, 2, :], 0.0, span_all[0:1, 3, :], ALU.max, ALU.subtract))
                    link(dve.tensor_scalar(excess[:, 2, :], excess[:, 2, :], -1.0, None, ALU.mult))
                    link(dve.tensor_reduce(most[:, :], excess[:, :, :], AX.XY, ALU.max))
                    dve.tensor_scalar(few[:, :], most[:, :], 0.0, None, ALU.is_le).then_inc(s_table, 1)

                dve.wait_ge(s_cols, 2)
                for n in range(H1 * NP):
                    h, (a, b) = n // NP, PIECES[n % NP]
                    if n < NT:
                        dve.wait_ge(s_vp, n + 1)
                        wait(dve, s_vlo, n - 1)
                        dve.tensor_tensor(v_now[:, n % 2, :, :].rearrange("p h c -> p (h c)"), bank[VB[n % 2]][0:TP, :],
                                          bv_sb[0:TP, :], ALU.add).then_inc(s_v, 1)
                    dve.wait_ge(s_k, 2 * n + 2)
                    dve.tensor_tensor(KT[:, h, 1, a:b], k_now[:, n % 2, 0:b - a], KT[:, h, 0, a:b],
                                      ALU.subtract).then_inc(s_klo, 1)
                    if n == 22:
                        tables()
                dve.wait_ge(s_const, 7)
                dve.wait_ge(s_cols, 2)
                dve.wait_ge(s_table, 2)

                def masks(w, u, v):
                    dve.wait_ge(s_log, NB * w + v + 1)
                    to = log[:, v, :].rearrange("p (a b) -> p a b", a=2)
                    dve.scalar_tensor_tensor(to, counts(u, v), -BIG, to, ALU.add, ALU.min).then_inc(s_masked, 1)

                def first_chunk(w):
                    return nc.s_assert_within(dve.value_load(first_i[0:1, bass.ds(w, 1)]), 0, NCH - 1,
                                              skip_runtime_bounds_check_because="a chunk's number")

                def relative_rows(w, u):
                    wait(dve, s_row_act, len(ROWS_BY_ACT) * w)
                    dve.tensor_scalar(minus_rel[:, u, :], row_of[:, bass.ds(first_chunk(w), KF)], base[:, bass.ds(w, 1)], -1.0,
                                      ALU.add, ALU.mult).then_inc(s_rel, 1)

                def window(w, u, masks_last):
                    c0 = first_chunk(w)
                    row_w, col_w = row_of[:, bass.ds(c0, KF)], col_of[:, bass.ds(c0, KF)]
                    for k in range(KF):
                        dve.wait_ge(s_hot_free, KF * w + k + 1)
                        if group_of(k) is None:
                            cut = rows_cut(k)
                            dve.tensor_scalar(row_hot(k), rows[:, cut], row_w[:, k:k + 1],
                                              base[:, bass.ds(w, 1)], ALU.subtract, ALU.is_equal)
                        dve.tensor_scalar(col_hot[:, k % RING, :], cols[:, :], col_w[:, k:k + 1], BIG,
                                          ALU.is_equal, ALU.mult).then_inc(s_hot, 1)
                        if masks_last and k in MASKS_AFTER:
                            masks(w - 1, 1 - u, MASKS_AFTER.index(k))
                        if k == NEXT_AFTER and not (isinstance(w, int) and w == NW - 1):
                            relative_rows(w + 1, 1 - u)

                is_few = dve.value_load(few[0:1, 0:1], min_val=0, max_val=1)
                with dve.If(is_few > 0):
                    relative_rows(0, 0)
                    window(0, 0, False)
                    with dve.Fori(0, NW // 2 - 1) as i:
                        window(2 * i + 1, 1, True)
                        window(2 * i + 2, 0, True)
                    window(NW - 1, 1, True)
                    for v in range(NB):
                        masks(NW - 1, 1, v)
                with dve.Else():
                    link(dve.tensor_scalar(end_c[:, :], end_c[:, :], 1.0, 1.0, ALU.max, ALU.add))
                    link(dve.tensor_copy(steps_i[:, :], end_c[:, :]))
                    link(dve.tensor_scalar(steps_i[:, :], steps_i[:, :], 1, None, ALU.arith_shift_right))
                    link(dve.tensor_copy(steps_f[:, :], steps_i[:, :]))
                    link(dve.tensor_tensor_scan(ends_cum[:, :], steps_f[:, :], zero_row[:, :], 0.0, ALU.add, ALU.add))
                    link(dve.tensor_tensor(starts_f[:, :], ends_cum[:, :], steps_f[:, :], ALU.subtract))
                    link(dve.scalar_tensor_tensor(offs_f[:, :], starts_f[:, :], -2.0, first_c[:, :], ALU.mult, ALU.add))
                    dve.tensor_copy(table[:, 0, :], starts_f[:, :]).then_inc(s_table, 1)
                    dve.tensor_copy(table[:, 1, :], ends_cum[:, :]).then_inc(s_table, 1)
                    dve.tensor_copy(table[:, 2, :], offs_f[:, :]).then_inc(s_table, 1)
                    dve.wait_ge(s_table, 5)
                    with dve.Fori(0, NW // 2) as i:
                        for par in range(2):
                            w = 2 * i + par
                            j0 = dve.value_load(table[0:1, 0, bass.ds(w, 1)], min_val=0, max_val=NCH * NW)
                            j1 = dve.value_load(table[0:1, 1, bass.ds(w, 1)], min_val=1, max_val=NCH * NW)
                            off = dve.value_load(table[0:1, 2, bass.ds(w, 1)], min_val=-2 * NCH * NW, max_val=NCH)
                            with dve.Fori(j0, j1) as j:
                                for u in range(2):
                                    c = nc.s_assert_within(2 * j + off + u, 0, NCH, skip_runtime_bounds_check_because=
                                                           "the table's chunks end at NCH, the first pad column")
                                    dve.wait_ge(s_hot_free, 2 * j + u + 1 + RING - 2)
                                    dve.tensor_scalar(row_pair[:, u, :], rows[:, :], row_of[:, bass.ds(c, 1)],
                                                      base[:, bass.ds(w, 1)], ALU.subtract, ALU.is_equal)
                                    dve.tensor_scalar(col_hot[:, u, :], cols[:, :], col_of[:, bass.ds(c, 1)], BIG,
                                                      ALU.is_equal, ALU.mult).then_inc(s_hot, 1)
                            for v in range(NB):
                                masks(w, par, v)

            @block.tensor
            def _(pe):
                pe.wait_ge(s_ident, 1)
                for n, (which, g0, g1) in enumerate(e_groups):
                    pe.wait_ge(s_list, 1 + which)
                    wait(pe, s_e, n - 1)
                    for g in range(g0, g1):
                        last = pe.transpose(bank[EB[n % 2]][0:CE, (g - g0) * CP:(g - g0 + 1) * CP],
                                            ends_f[:, which, g * CE:(g + 1) * CE], ident[0:CP, 0:CP])
                    last.then_inc(s_ep, 1)
                pe.wait_ge(s_x, 16)
                pe.wait_ge(s_e, len(e_groups))
                for n, g in enumerate(x_groups):
                    wait(pe, s_xt, n - 1)
                    for t in g:
                        last = pe.transpose(bank[EB[n % 2]][:, (t - g[0]) * TP:(t - g[0] + 1) * TP],
                                            xres[:, t, :], ident[0:TP, 0:TP])
                    last.then_inc(s_xtp, 1)
                pe.wait_ge(s_xt, len(x_groups))
                scales.bounds(pe)
                scales.columns(pe)
                scales.wait_weights(pe)
                xT_all = xT[:, :, 0, :].rearrange("c t n -> c (t n)")
                for n in range(H1 * NP):
                    h, (a, b) = n // NP, PIECES[n % NP]
                    wait(pe, s_k, 2 * (n - 1))
                    pe.matmul(bank[KB[n % 2]][:, 0:b - a], Wk_sb[:, 0, h * C:(h + 1) * C], xT_all[:, a:b],
                              start=True, stop=True).then_inc(s_kp, 1)
                    if n < NT:
                        wait(pe, s_v, n - 1)
                        pe.matmul(bank[VB[n % 2]][0:TP, :], xT[:, n, 0, :], Wv_sb[:, 0, :],
                                  start=True, stop=True).then_inc(s_vp, 1)
                pe.wait_ge(s_k, 2 * H1 * NP)
                pe.wait_ge(s_v, NT)
                pe.wait_ge(s_table, 2)

                def product(u, hot, rows_of, k=None):
                    for v, one_hot in rows_of:
                        for a in range(2):
                            ins = pe.matmul(counts(u, v)[:, a, :], one_hot,
                                            col_hot[:, hot, a * HB:(a + 1) * HB], start=k == (0, KF1)[v], stop=False,
                                            skip_group_check=True)
                    ins.then_inc(s_hot_free, 1)

                def add_zeros(u, width, first):
                    for v in range(NB):
                        for a in range(2):
                            ins = pe.matmul(counts(u, v)[:, a, 0:width], zeros[:, 0:TP], zeros[:, 0:width], start=first,
                                            stop=not first, skip_group_check=True)
                    return ins

                is_few = pe.value_load(few[0:1, 0:1], min_val=0, max_val=1)
                with pe.If(is_few > 0):
                    with pe.Fori(0, NW // 2) as i:
                        for u in range(2):
                            w = 2 * i + u
                            pe.wait_ge(s_masked, NB * w + NB)
                            for k in range(KF):
                                pe.wait_ge(s_hot, KF * w + k + 1)
                                if group_of(k) is not None:
                                    pe.wait_ge(s_row_act, len(ROWS_BY_ACT) * (w + 1) + group_of(k) + 1)
                                product(u, k % RING, [(v, row_hot(k, v)) for v in blocks_of(k)], k)
                            add_zeros(u, 1, False).then_inc(s_cnt, 1)
                with pe.Else():
                    pe.wait_ge(s_table, 5)
                    with pe.Fori(0, NW // 2) as i:
                        for u in range(2):
                            w = 2 * i + u
                            j0 = pe.value_load(table[0:1, 0, bass.ds(w, 1)], min_val=0, max_val=NCH * NW)
                            j1 = pe.value_load(table[0:1, 1, bass.ds(w, 1)], min_val=1, max_val=NCH * NW)
                            pe.wait_ge(s_masked, NB * w + NB)
                            add_zeros(u, HB, True)
                            with pe.Fori(j0, j1) as j:
                                for hot in range(2):
                                    pe.wait_ge(s_hot, 2 * j + hot + 1)
                                    product(u, hot, [(v, row_pair[:, hot, v * TP:(v + 1) * TP]) for v in range(NB)])
                            add_zeros(u, 1, False).then_inc(s_cnt, 1)


def projections2(nc, Wk, bk, Wv, bv, Wq, bq, Ws, L, hT_dram, h_max, ident):
    hT, KT, V = L["featT"], L["KT"], L["V"]
    with ExitStack() as ctx:
        def sb(name, shape, dt=F32):
            return ctx.enter_context(nc.sbuf_tensor(name, shape, dt))

        def sem(name):
            return ctx.enter_context(nc.semaphore(name))

        Wk_sb, Wv_sb = sb("Wk2_sb", [C, H1, H2 * C]), sb("Wv2_sb", [C, H1, H2 * C])
        bk_sb, bv_sb = sb("bk2_sb", [C, H2]), sb("bv2_sb", [C, H2 * C])
        up = sb("scale_up2", [C, 3, H2 * C])
        abs_w = sb("abs_w2", [C, 3, H1, H2 * C])
        k_now, v_now = sb("k_now2", [C, 2, PW]), sb("v_now2", [TP, 2, H2, C])
        bank = [ctx.enter_context(nc.psum_tensor(f"proj_bank{i}", [C, 512], F32)) for i in range(5)]
        s_h = [sem(f"h_loaded{p}") for p in range(NP)]
        s_w, s_bias, s_late = sem("w2_loaded"), sem("bias2_loaded"), sem("late2_loaded")
        s_kp, s_k = sem("key2_in_psum"), sem("key2_ready")
        s_vp, s_v = sem("value2_in_psum"), sem("value2_ready")
        s_klo, s_vhi, s_vlo = sem("key2_lo_ready"), sem("value2_hi_ready"), sem("value2_lo_ready")
        s_rows, s_dve = sem("bias2_rows_loaded"), sem("dve_chain2")
        scales = Scales(nc, sb, sem, 2, H2, H1, (Wk_sb, L["Wq"], Wv_sb), bv_sb,
                        (bk_sb, L["bq"]), L["v_back"], abs_w, up, bank, ident)

        with nc.Block() as block:
            @block.sync
            def _(sp):
                sp.dma_start(Wk_sb[:, :, :], Wk.rearrange("(k c) n -> c k n", c=C)).then_inc(s_w, 16)
                sp.dma_start(L["Wq"][:, :, :], Wq.rearrange("(k c) n -> c k n", c=C)).then_inc(s_w, 16)
                sp.dma_start(Wv_sb[:, :, :], Wv.rearrange("(k c) n -> c k n", c=C)).then_inc(s_w, 16)
                for i, b in enumerate((bk, bq)):
                    sp.dma_start(scales.abs_rows[:, i, :], b.partition_broadcast(C)).then_inc(s_rows, 16)
                sp.dma_start(bv_sb[:, :], bv.partition_broadcast(C)).then_inc(s_rows, 16)
                for p in range(NP):
                    t0, t1 = tiles_of(p)[0], tiles_of(p)[-1] + 1
                    sp.dma_start(hT[:, t0:t1, :, :].rearrange("c t h n -> c t (h n)"),
                                 hT_dram[t0:t1].rearrange("t c n -> c t n")).then_inc(s_h[p], 16)

            @block.scalar
            def _(act):
                with nc.allow_non_contiguous_dma("small bias columns"):
                    act.dma_start(bk_sb[:, :], bk.rearrange("(h c) -> c h", c=C)).then_inc(s_bias, 16)
                    act.dma_start(L["bq"][:, :], bq.rearrange("(h c) -> c h", c=C)).then_inc(s_bias, 16)
                act.dma_start(L["Ws"][:, :, :], Ws.rearrange("(k c) n -> c k n", c=C)).then_inc(s_late, 16)
                act.wait_ge(s_w, 48)
                act.wait_ge(s_rows, 48)
                scales.magnitudes(act)
                scales.root(act)
                scales.wait_scaled(act)
                for n in range(H2 * NP):
                    h, (a, b) = n % H2, PIECES[n // H2]
                    act.wait_ge(s_kp, n + 1)
                    wait(act, s_klo, n - 1)
                    for to in (k_now[:, n % 2, 0:b - a], KT[:, h, 0, a:b]):
                        act.activation(to, bank[n % 2][:, 0:b - a], ACT.Identity, bias=bk_sb[:, h:h + 1]).then_inc(s_k, 1)
                act.wait_ge(s_late, 16)

            @block.gpsimd
            def _(pool):
                for t in range(NT):
                    pool.wait_ge(s_v, t + 1)
                    pool.tensor_copy(V[:, t, :, 0, :], v_now[:, t % 2, :, :]).then_inc(s_vhi, 1)

            @block.vector
            def _(dve):
                chain = [0]

                def link(ins, sem=None):
                    chain[0] += sem is None
                    ins.then_inc(sem or s_dve, 1)
                    dve.wait_ge(sem or s_dve, chain[0] if sem is None else 1)

                scales.largest(dve, link, h_max[:, :, :, :])
                dve.wait_ge(s_bias, 32)
                scales.scale(dve, link)
                def value_low(t):
                    dve.wait_ge(s_vhi, t + 1)
                    dve.tensor_tensor(V[:, t, :, 1, :], v_now[:, t % 2, :, :], V[:, t, :, 0, :], ALU.subtract).then_inc(s_vlo, 1)

                n = 0
                for p, (a, b) in enumerate(PIECES):
                    for h in range(H2):
                        dve.wait_ge(s_k, 2 * n + 2)
                        dve.tensor_tensor(KT[:, h, 1, a:b], k_now[:, n % 2, 0:b - a], KT[:, h, 0, a:b],
                                          ALU.subtract).then_inc(s_klo, 1)
                        n += 1
                    for t in tiles_of(p):
                        dve.wait_ge(s_vp, t + 1)
                        wait(dve, s_vlo, t - 1)
                        dve.tensor_tensor(v_now[:, t % 2, :, :].rearrange("p h c -> p (h c)"),
                                          bank[2 + t % 2][0:TP, 0:H2 * C], bv_sb[0:TP, :], ALU.add).then_inc(s_v, 1)
                        if t > 0:
                            value_low(t - 1)
                value_low(NT - 1)

            @block.tensor
            def _(pe):
                scales.bounds(pe)
                scales.columns(pe)
                scales.wait_weights(pe)
                n = 0
                for p, (a, b) in enumerate(PIECES):
                    pe.wait_ge(s_h[p], 16)
                    t0, t1 = tiles_of(p)[0], tiles_of(p)[-1] + 1
                    for h in range(H2):
                        wait(pe, s_k, 2 * (n - 1))
                        for k in range(H1):
                            last = pe.matmul(bank[n % 2][:, 0:b - a], Wk_sb[:, k, h * C:(h + 1) * C],
                                             hT[:, t0:t1, k, :], start=k == 0, stop=k == H1 - 1)
                        last.then_inc(s_kp, 1)
                        n += 1
                    for t in tiles_of(p):
                        wait(pe, s_v, t - 1)
                        for k in range(H1):
                            last = pe.matmul(bank[2 + t % 2][0:TP, 0:H2 * C], hT[:, t, k, :], Wv_sb[:, k, :],
                                             start=k == 0, stop=k == H1 - 1)
                        last.then_inc(s_vp, 1)


def attention(nc, layer, H, KC, L, mask_dram, ident, hT_dram=None, h_max=None, xres=None, y=None, stats=None):
    featT, KT, V, v_back, Wq, Ws, bq = (L[n] for n in ("featT", "KT", "V", "v_back", "Wq", "Ws", "bq"))
    W = H * C if layer == 1 else C
    with ExitStack() as ctx:
        def sb(name, shape, dt=F32):
            return ctx.enter_context(nc.sbuf_tensor(f"{name}_l{layer}", shape, dt))

        def bank(name):
            return ctx.enter_context(nc.psum_tensor(f"{name}_l{layer}", [C, 512], F32))

        def sem(name):
            return ctx.enter_context(nc.semaphore(f"{name}_l{layer}"))

        q_now = sb("q_now", [C, 2, TP])
        QT = sb("QT", [C, 2, 2, TP], F16)
        bq_s = sb("bq_scaled", [C, H])
        mask = sb("mask", [TP, 2, N])
        prob = sb("prob", [TP, 2, N])
        probT = sb("probT", [TP, NP, 2, PW], F16)
        feat_now = sb("feat_now", [C, KC, TP])
        skip = sb("skip", [TP, W])
        rows = sb("rows", [TP, W])
        rowsT = sb("rowsT", [C, H * TP])
        piece_max = sb("piece_max", [TP, 2, NP])
        neg_max = sb("neg_max", [TP, 2])
        total = sb("total", [TP, 2, len(EXP_PARTS)])
        all_total = sb("all_total", [TP, 1])
        denom, inv, weight = sb("denom", [TP, 1]), sb("inv", [TP, 1]), sb("weight", [TP, 2])
        summed = sb("summed", [TP, 2, C])

        S = [bank(f"score{i}") for i in range(3)]
        T = [bank(f"transposed{i}") for i in range(2)]
        O, B_q, B_skip = bank("output"), bank("query"), bank("skip_rows")

        s_mask = [sem("mask_even_loaded"), sem("mask_odd_loaded")]
        s_feat = sem("feat_ready")
        s_bq = sem("query_bias_ready")
        s_qp, s_qs, s_qh, s_q = (sem(n) for n in ("query_in_psum", "query_scaled", "query_hi_ready", "query_ready"))
        s_score, s_seen, s_masked = sem("score_ready"), sem("score_seen"), sem("score_masked")
        s_max, s_exp = sem("max_ready"), sem("exp_ready")
        s_tp, s_hi, s_t = sem("transposed_in_psum"), sem("probT_hi_ready"), sem("probT_ready")
        s_pv = sem("values_summed")
        s_sum, s_back, s_wtd, s_out = (sem(n) for n in ("sum_ready", "sum_scaled_back", "sum_weighted", "rows_ready"))
        s_low, s_pool_seen, s_top = sem("sum_low_ready"), sem("pool_seen"), sem("largest_taken")
        s_sp, s_skip = sem("skip_in_psum"), sem("skip_ready")
        s_rp, s_r, s_stored = sem("rowsT_in_psum"), sem("rowsT_ready"), sem("rowsT_stored")
        s_tot, s_w0, s_w1, s_w2 = (sem(n) for n in ("total_ready", "denom_ready", "inverse_ready", "weight_ready"))
        EP = len(EXP_PARTS)
        FIRST = ((0, PIECES[1][1]), (PIECES[1][1], N))
        s_first = [sem("mask_first_a"), sem("mask_first_b")]
        def over_tiles(eng, body):
            body(0, 0, 0)
            with eng.Fori(0, (NT - 3) // 2) as i:
                body(2 * i + 1, i, 1)
                body(2 * i + 2, i + 1, 0)
            body(NT - 2, (NT - 2) // 2, 1)
            body(NT - 1, (NT - 1) // 2, 0)

        def is_first(t):
            return isinstance(t, int) and t == 0

        def exists(t):
            return not isinstance(t, int) or t < NT

        def ahead(t, h, n):
            return t + (h + n) // H, (h + n) % H

        def score_bank(h, p):
            return S[(p + h % 2) % 3]

        def score_bank_back(h, p):
            banks = [(q + g) % 3 for g in range(2) for q in range(NP)]
            n = h % 2 * NP + p
            return next(d for d in range(1, len(banks)) if banks[n - d] == banks[n])

        def flip_bank(h, p):
            return T[(h * NP + p) % 2]

        with nc.Block() as block:
            @block.sync
            def _(sp):
                def load_mask(t, parity):
                    for r0, r1 in ROW_SPLIT:
                        sp.dma_start(mask[r0:r1, parity, :], mask_dram[bass.ds(t * TP + r0, r1 - r0), :]
                                     ).then_inc(s_mask[parity], 16)

                def store_rowsT(t):
                    sp.wait_ge(s_r, t + 1)
                    sp.dma_start(hT_dram[bass.ds(t, 1)].rearrange("a p n -> (a p) n"), rowsT[:, :]).then_inc(s_stored, 16)

                def tile(t, i, parity):
                    if exists(t + 2):
                        sp.wait_ge(s_masked, NP * H * (t + 1))
                        load_mask(t + 2, parity)
                    if layer == 1:
                        store_rowsT(t)

                for n, (a, b) in enumerate(FIRST):
                    for r0, r1 in ROW_SPLIT:
                        sp.dma_start(mask[r0:r1, 0, a:b], mask_dram[r0:r1, a:b]).then_inc(s_first[n], 16)
                load_mask(1, 1)
                over_tiles(sp, tile)
                if layer == 1:
                    sp.wait_ge(s_stored, 16 * NT)

            @block.gpsimd
            def _(pool):
                def query_parts(n, u):
                    pool.wait_ge(s_qs, n + 1).then_inc(s_pool_seen, 1)
                    pool.tensor_copy(QT[:, u, 0, :], q_now[:, u, :]).then_inc(s_qh, 1)
                    pool.wait_ge(s_qh, n + 1)
                    pool.tensor_tensor(QT[:, u, 1, :], q_now[:, u, :], QT[:, u, 0, :], ALU.subtract).then_inc(s_q, 1)

                def tile(t, i, parity):
                    wait(pool, s_sp, t)
                    pool.tensor_copy(feat_now[:, :, :].rearrange("c k n -> c (k n)"),
                                     featT[:, bass.ds(t, 1), :, :].rearrange("c a k n -> c (a k n)")).then_inc(s_feat, 1)
                    for h in range(H):
                        s = t * H + h
                        if exists(ahead(t, h, 3)[0]):
                            query_parts(s + 3, (h + 3) % 2)
                        o = summed[:, h % 2, :]
                        pool.wait_ge(s_sum, s + 1)
                        pool.tensor_tensor(o, o, v_back[0:TP, h * C:(h + 1) * C], ALU.mult).then_inc(s_back, 1)
                        pool.wait_ge(s_w2, s + 1)
                        pool.wait_ge(s_back, s + 1).then_inc(s_pool_seen, 1)
                        pool.tensor_scalar(o, o, weight[:, h % 2:h % 2 + 1], None, ALU.mult).then_inc(s_wtd, 1)
                        pool.wait_ge(s_skip, t + 1)
                        pool.wait_ge(s_wtd, s + 1)
                        if layer == 1:
                            if h == 0:
                                wait(pool, s_rp, t)
                            pool.tensor_tensor(rows[:, h * C:(h + 1) * C], o, skip[:, h * C:(h + 1) * C],
                                               ALU.add).then_inc(s_out, 1)
                        elif h == 0:
                            pool.tensor_tensor(rows[:, :], o, skip[:, :], ALU.add).then_inc(s_out, 1)
                        else:
                            pool.wait_ge(s_out, s)
                            pool.tensor_tensor(y[:, bass.ds(t, 1), :].rearrange("p a c -> p (a c)"), o, rows[:, :],
                                               ALU.add).then_inc(s_out, 1)

                for n in range(3):
                    query_parts(n, n % 2)
                over_tiles(pool, tile)

            @block.scalar
            def _(act):
                def query(n, h):
                    act.wait_ge(s_qp, n + 1)
                    act.activation(q_now[:, h % 2, :], B_q[:, 0:TP], ACT.Identity, bias=bq_s[:, h:h + 1],
                                   scale=SCALE).then_inc(s_qs, 1)

                def rows_transposed(t):
                    act.wait_ge(s_rp, t + 1)
                    wait(act, s_stored, 16 * t)
                    wait(act, s_top, t)
                    act.activation(rowsT[:, :], B_skip[:, 0:H * TP], ACT.Relu).then_inc(s_r, 1)

                def exponentials(s, h, c):
                    if c == 0:
                        act.wait_ge(s_max, s + 1)
                    e = prob[:, h % 2, PIECES[EXP_PARTS[c][0]][0]:PIECES[EXP_PARTS[c][-1]][1]]
                    act.activation(e, e, ACT.Exp, bias=neg_max[:, h % 2:h % 2 + 1],
                                   accum_out=total[:, h % 2, c:c + 1]).then_inc(s_exp, 1)

                def high_part(s, h, p):
                    a, b = PIECES[p]
                    act.wait_ge(s_tp, NP * s + p + 1)
                    wait(act, s_pv, NP * (s - 1) + p + 1)
                    act.activation(probT[:, p, 0, 0:b - a], flip_bank(h, p)[0:TP, 0:b - a], ACT.Copy,
                                   scale=P_UP).then_inc(s_hi, 1)

                def tile(t, i, parity):
                    for h in range(H):
                        s = t * H + h
                        for k in range(NP):
                            n, p = divmod(k + 2, NP)
                            tn, hn = ahead(t, h, n)
                            if exists(tn):
                                high_part(s + n, hn, p)
                            c, (tn, hn) = k - 2, ahead(t, h, 1)
                            if c in range(EP) and exists(tn):
                                exponentials(s + 1, hn, c)
                            tn, hn = ahead(t, h, 3)
                            if k == 3 and exists(tn):
                                query(s + 3, hn)
                            if layer == 1 and h == 0 and k == 3 and not is_first(t):
                                rows_transposed(t - 1)

                act.mul(bq_s[:, :], bq[:, :], SCALE).then_inc(s_bq, 1)
                act.wait_ge(s_bq, 1)
                for n in range(3):
                    query(n, n % H)
                for c in range(EP):
                    exponentials(0, 0, c)
                for q in range(2):
                    high_part(0, 0, q)
                over_tiles(act, tile)
                if layer == 1:
                    rows_transposed(NT - 1)

            @block.vector
            def _(dve):
                def masked_scores(s, h, p, i, parity):
                    a, b = PIECES[p]
                    first_tile = isinstance(s, int) and s == 0
                    for n, cols in enumerate(FIRST):
                        if first_tile and a == cols[0]:
                            dve.wait_ge(s_first[n], 16 * len(ROW_SPLIT))
                    if p == 0:
                        wait(dve, s_max, s - 1)
                        if h == 0 and not first_tile:
                            dve.wait_ge(s_mask[parity], 16 * len(ROW_SPLIT) * (i + parity))
                    dve.wait_ge(s_score, NP * s + p + 1).then_inc(s_seen, 1)
                    dve.tensor_tensor_reduce(out=prob[:, h % 2, a:b], in0=score_bank(h, p)[0:TP, 0:b - a], in1=mask[:, parity, a:b],
                                             scale=1.0, scalar=-3.0e38, op0=ALU.add, op1=ALU.max,
                                             accum_out=piece_max[:, h % 2, p:p + 1]).then_inc(s_masked, 1)
                    if p == NP - 1:
                        dve.wait_ge(s_masked, NP * (s + 1))
                        wait(dve, s_w2, s - 1)
                        dve.tensor_reduce(neg_max[:, h % 2:h % 2 + 1], piece_max[:, h % 2, :], AX.X, ALU.max,
                                          negate=True).then_inc(s_max, 1)

                def low_part(s, h, p):
                    a, b = PIECES[p]
                    dve.wait_ge(s_hi, NP * s + p + 1)
                    dve.scalar_tensor_tensor(probT[:, p, 1, 0:b - a], flip_bank(h, p)[0:TP, 0:b - a], P_UP,
                                             probT[:, p, 0, 0:b - a], ALU.mult, ALU.subtract).then_inc(s_t, 1)

                def weights(s, h, k):
                    if k == 1:
                        dve.wait_ge(s_exp, EP * (s + 1))
                        dve.tensor_reduce(all_total[:, :], total[:, h % 2, :], AX.X, ALU.add).then_inc(s_tot, 1)
                    if k == 2:
                        dve.wait_ge(s_tot, s + 1)
                        dve.tensor_scalar(denom[:, :], all_total[:, :], 1.0 if layer == 1 else float(H2),
                                          EPS_DENOM, ALU.mult, ALU.add).then_inc(s_w0, 1)
                    if k == 3:
                        dve.wait_ge(s_w0, s + 1)
                        dve.reciprocal(inv[:, :], denom[:, :]).then_inc(s_w1, 1)
                    if k == 4:
                        dve.wait_ge(s_w1, s + 1)
                        wait(dve, s_wtd, s - 1)
                        dve.scalar_tensor_tensor(weight[:, h % 2:h % 2 + 1], neg_max[:, h % 2:h % 2 + 1], NO_EDGE, inv[:, :],
                                                 ALU.is_lt, ALU.mult).then_inc(s_w2, 1)

                def value_sum(s, h):
                    dve.wait_ge(s_pv, NP * (s + 1))
                    wait(dve, s_out, s - 1)
                    dve.tensor_copy(summed[:, h % 2, :], O[0:TP, C:2 * C]).then_inc(s_low, 1)
                    dve.wait_ge(s_low, s + 1)
                    dve.tensor_tensor(summed[:, h % 2, :], O[0:TP, 0:C], summed[:, h % 2, :], ALU.add).then_inc(s_sum, 1)

                def largest_features(t):
                    dve.wait_ge(s_r, t + 1)
                    dve.tensor_reduce(h_max[:, :, bass.ds(t, 1), 0], rowsT[:, :].rearrange("c (k n) -> c k n", k=H),
                                      AX.X, ALU.max).then_inc(s_top, 1)

                def tile(t, i, parity):
                    for h in range(H):
                        s = t * H + h
                        for k in range(NP):
                            n, p = divmod(k + LEAD, NP)
                            tn, hn = ahead(t, h, n + 1)
                            if exists(tn):
                                on = (h + n + 1) // H
                                masked_scores(s + n + 1, hn, p, i + (parity + on) // 2, (parity + on) % 2)
                            if k == NP - 1:
                                value_sum(s, h)
                            n, p = divmod(k + 2, NP)
                            tn, hn = ahead(t, h, n)
                            if exists(tn):
                                low_part(s + n, hn, p)
                            weights(s, h, k)
                            if k == 4 and layer == 2 and h == 0 and not is_first(t):
                                dve.wait_ge(s_out, s)
                                dve.bn_stats(stats[:, bass.ds(t - 1, 1), :].rearrange("p a c -> p (a c)"),
                                             y[:, bass.ds(t - 1, 1), :].rearrange("p a c -> p (a c)"))
                            if layer == 1 and k == 4 and h == 0 and not is_first(t):
                                largest_features(t - 1)
                            if k == NP - 1 and h == 0:
                                dve.wait_ge(s_sp, t + 1)
                                wait(dve, s_out, s)
                                add = L["bs"][:, :] if layer == 1 else xres[:, bass.ds(t, 1), :].rearrange("p a c -> p (a c)")
                                dve.tensor_tensor(skip[:, :], B_skip[0:TP, 0:W], add, ALU.add).then_inc(s_skip, 1)

                for q in range(NP):
                    masked_scores(0, 0, q, 0, 0)
                for q in range(LEAD):
                    masked_scores(1, 1, q, 0, 0)
                for q in range(2):
                    low_part(0, 0, q)
                over_tiles(dve, tile)
                if layer == 1:
                    largest_features(NT - 1)
                if layer == 2:
                    dve.wait_ge(s_out, H * NT)
                    dve.bn_stats(stats[:, NT - 1, :], y[:, NT - 1, :])

            @block.tensor
            def _(pe):
                def query(n, t, h):
                    wait(pe, s_qs, n)
                    for k in range(KC):
                        last = pe.matmul(B_q[:, 0:TP], Wq[:, k, h * C:(h + 1) * C],
                                         featT[:, bass.ds(t, 1), k, :].rearrange("c a n -> c (a n)"),
                                         start=k == 0, stop=k == KC - 1)
                    last.then_inc(s_qp, 1)

                def scores(s, h, p):
                    if p == 0:
                        pe.wait_ge(s_q, s + 1)
                    a, b = PIECES[p]
                    wait(pe, s_masked, NP * s + p + 1 - score_bank_back(h, p))
                    parts = ((0, 0), (0, 1), (1, 0))
                    for n, (i, j) in enumerate(parts):
                        last = pe.matmul(score_bank(h, p)[0:TP, 0:b - a], QT[:, h % 2, i, :], KT[:, h, j, a:b],
                                         start=n == 0, stop=n == len(parts) - 1)
                    last.then_inc(s_score, 1)

                def skip_product(t):
                    pe.wait_ge(s_feat, t + 1)
                    if layer == 1:
                        wait(pe, s_r, t)
                    else:
                        wait(pe, s_skip, t)
                    for k in range(KC):
                        last = pe.matmul(B_skip[0:TP, 0:W], feat_now[:, k, :], Ws[:, k, :], start=k == 0, stop=k == KC - 1)
                    last.then_inc(s_sp, 1)

                def rows_transposed(t):
                    pe.wait_ge(s_out, H * (t + 1))
                    for h in range(H):
                        last = pe.transpose(B_skip[:, h * TP:(h + 1) * TP], rows[:, h * C:(h + 1) * C], ident[0:TP, 0:TP])
                    last.then_inc(s_rp, 1)

                def transposes(s, p, h):
                    wait(pe, s_t, NP * s + p - 1)
                    c = next(c for c, pieces in enumerate(EXP_PARTS) if p in pieces)
                    pe.wait_ge(s_exp, EP * s + c + 1)
                    for i, t in enumerate(tiles_of(p)):
                        last = pe.transpose(flip_bank(h, p)[0:TP, i * TP:(i + 1) * TP], prob[:, h % 2, t * TP:(t + 1) * TP],
                                            ident[0:TP, 0:TP])
                    last.then_inc(s_tp, 1)

                def values(s, p, h):
                    pe.wait_ge(s_t, NP * s + p + 1)
                    if p == 0:
                        wait(pe, s_sum, s)
                    for i, t in enumerate(tiles_of(p)):
                        hi, lo = (probT[:, p, n, i * TP:(i + 1) * TP] for n in range(2))
                        pe.matmul(O[0:TP, 0:2 * C], hi, V[:, t, h, :, :].rearrange("p a c -> p (a c)"),
                                  start=t == 0, stop=False, skip_group_check=True)
                        last = pe.matmul(O[0:TP, 0:C], lo, V[:, t, h, 0, :], start=False, stop=t == NT - 1,
                                         skip_group_check=True)
                    last.then_inc(s_pv, 1)

                def tile(t, i, parity):
                    for h in range(H):
                        s = t * H + h
                        for k in range(NP):
                            n, p = divmod(k + LEAD, NP)
                            tn, hn = ahead(t, h, n + 1)
                            if exists(tn):
                                scores(s + n + 1, hn, p)
                            n, p = divmod(k + 2, NP)
                            tn, hn = ahead(t, h, n)
                            if exists(tn):
                                transposes(s + n, p, hn)
                            values(s, k, h)
                            tn, hn = ahead(t, h, 3)
                            if k == 3 and exists(tn):
                                query(s + 3, tn, hn)
                            if layer == 1 and k == 3 and h == 0 and not is_first(t):
                                rows_transposed(t - 1)
                            if k == 5 and h == 0:
                                skip_product(t)

                query(0, 0, 0)
                query(1, 0, 1)
                for q in range(NP):
                    scores(0, 0, q)
                query(2, *ahead(0, 0, 2))
                for q in range(LEAD):
                    scores(1, 1, q)
                for q in range(2):
                    transposes(0, q, 0)
                over_tiles(pe, tile)
                if layer == 1:
                    rows_transposed(NT - 1)


def layer_norm(nc, y, stats, out):
    groups = [range(a, min(a + 7, NT)) for a in range(0, NT, 7)]
    with ExitStack() as ctx:
        moments = ctx.enter_context(nc.sbuf_tensor("moments", [TP, NT, 2], F32))
        dev = ctx.enter_context(nc.sbuf_tensor("dev", [TP, NT], F32))
        eps = ctx.enter_context(nc.sbuf_tensor("eps", [TP, 1], F32))
        s_eps, s_mom, s_dev, s_inv, s_y, s_outd = (ctx.enter_context(nc.semaphore(n)) for n in
                                             ("eps_ready", "moments_ready", "dev_ready", "inv_dev_ready", "y_ready", "out_stored"))
        with nc.Block() as block:
            @block.vector
            def _(dve):
                dve.memset(eps[:, :], EPS_NORM).then_inc(s_eps, 1)
                for t in range(NT):
                    dve.bn_aggr(moments[:, t, :], stats[:, t, :]).then_inc(s_mom, 1)
                dve.wait_ge(s_dev, 1)
                dve.reciprocal(dev[:, :], dev[:, :]).then_inc(s_inv, 1)
                dve.wait_ge(s_inv, 1)
                for t in range(NT):
                    dve.tensor_scalar(y[:, t, :], y[:, t, :], moments[:, t, 0:1], dev[:, t:t + 1],
                                      ALU.subtract, ALU.mult).then_inc(s_y, 1)

            @block.scalar
            def _(act):
                act.wait_ge(s_eps, 1)
                act.wait_ge(s_mom, NT)
                act.activation(dev[:, :], moments[:, :, 1], ACT.Sqrt, bias=eps[:, 0:1]).then_inc(s_dev, 1)

            @block.sync
            def _(sp):
                for g in groups:
                    sp.wait_ge(s_y, g[-1] + 1)
                    sp.dma_start(out.rearrange("(t p) c -> p t c", p=TP)[:, g[0]:g[-1] + 1, :], y[:, g[0]:g[-1] + 1, :]
                                 ).then_inc(s_outd, 16)
                sp.wait_ge(s_outd, 16 * len(groups))


_INS = ["x", "src", "dst"] + ["L0_gnn_" + a + b + n for n in "12" for a, b in
                              (("W", "q"), ("b", "q"), ("W", "k"), ("b", "k"), ("W", "v"), ("b", "v"), ("W", "s"), ("b", "s"))]


def kernel(**inputs):
    import numpy as _np
    import concourse.bacc as _bacc
    from concourse import mybir as _mybir
    from concourse.bass_utils import run_bass_kernel_spmd as _run

    nc = _bacc.Bacc("TRN2", target_bir_lowering=False, num_devices=1)
    arrays, args = {}, []
    for name in _INS:
        a = _np.ascontiguousarray(inputs[name])
        arrays[f"in_{name}"] = a
        args.append(nc.dram_tensor(f"in_{name}", a.shape, _mybir.dt.from_np(a.dtype), kind="ExternalInput").ap())
    args.append(nc.dram_tensor("out", (N, C), F32, kind="ExternalOutput").ap())
    build(nc, *args)
    r = _run(nc, [arrays], core_ids=[0])
    return r.results[0]["out"]
```
